# Optimizing a Trainium2 kernel written in Bass

```python
import numpy as np
import jax
import jax.numpy as jnp

def _softmax(x, axis=-1):
    return jax.nn.softmax(x, axis=axis)

def _gelu(x):
    return jax.nn.gelu(x, approximate=True)

def _silu(x):
    return jax.nn.silu(x)

def _sigmoid(x):
    return jax.nn.sigmoid(x)

def _layernorm(x, axis=-1, eps=1e-05):
    m = jnp.mean(x, axis=axis, keepdims=True)
    v = jnp.var(x, axis=axis, keepdims=True)
    return (x - m) / jnp.sqrt(v + eps)

def _scatter_add(tgt, idx, src, axis=0):
    return tgt.at[idx].add(src)

def _segment_sum(src, seg, n):
    return jax.ops.segment_sum(src, seg, n)
kernel_name = 'mk_lm_tower_d1_tok_ids1024_r4_e623d8'

def setup_inputs(seed: int=0):
    np.random.seed(seed)
    _w = jnp.asarray

    def _rec_inputs():
        import jax
        import jax.numpy as jnp
        _rk = jax.random.key(seed)
        x = jax.random.randint(jax.random.fold_in(_rk, 1), (16, 128), 0, 30521, jnp.int32)
        mask_BS_i1_0 = jnp.where(jnp.ones((16, 128), dtype=bool), 1, 0).astype(jnp.int32)
        return (x, mask_BS_i1_0)
    x, mask_BS_i1_0 = _rec_inputs()

    def _L0_tok_setup():
        import jax, jax.numpy as jnp
        import numpy as np
        EPS = 1e-05
        key = jax.random.key(seed)
        ks = jax.random.split(key, 5)
        B, S, V, H, P, T = (32, 128, 30522, 256, 128, 2)
        input_ids = jax.random.randint(ks[0], (B, S), 0, V)
        token_type_ids = jax.random.randint(ks[1], (B, S), 0, T)
        token_W = jax.random.normal(ks[2], (V, H), dtype=jnp.float32)
        pos_W = jax.random.normal(ks[3], (P, H), dtype=jnp.float32)
        type_W = jax.random.normal(ks[4], (T, H), dtype=jnp.float32)
        ln_w = jnp.ones((H,), dtype=jnp.float32)
        ln_b = jnp.zeros((H,), dtype=jnp.float32)
        return {'input_ids': input_ids, 'token_type_ids': token_type_ids, 'token_W': token_W, 'pos_W': pos_W, 'type_W': type_W, 'ln_w': ln_w, 'ln_b': ln_b}
    _L0_tok_all = _L0_tok_setup()
    _L0_tok_in = {k: v for k, v in _L0_tok_all.items() if k in ('token_W', 'pos_W', 'type_W', 'ln_w', 'ln_b')}
    del _L0_tok_all

    def _L0_attn_setup():
        import jax, jax.numpy as jnp
        import numpy as np
        D_MODEL = 256
        N_HEADS = 16
        HEAD_D = D_MODEL // N_HEADS
        B, T = (4, 1024)
        ROPE_BASE = 10000.0

        def _rope(x):
            Bx, Tx, Dx = x.shape
            half = Dx // 2
            inv_freq = 1.0 / ROPE_BASE ** (jnp.arange(half, dtype=jnp.float32) / half)
            ang = jnp.arange(Tx, dtype=jnp.float32)[:, None] * inv_freq[None, :]
            cos, sin = (jnp.cos(ang), jnp.sin(ang))
            x1 = x[..., 0::2]
            x2 = x[..., 1::2]
            r1 = x1 * cos - x2 * sin
            r2 = x1 * sin + x2 * cos
            out = jnp.stack([r1, r2], axis=-1).reshape(Bx, Tx, Dx)
            return out
        key = jax.random.key(seed)
        k_x, k_q, k_k, k_v = jax.random.split(key, 4)
        x = jax.random.normal(k_x, (B, T, D_MODEL), dtype=jnp.float32)
        bound = np.sqrt(6.0 / (HEAD_D * N_HEADS))
        shp = (HEAD_D, HEAD_D, N_HEADS)
        w_q = jax.random.uniform(k_q, shp, jnp.float32, -bound, bound)
        w_k = jax.random.uniform(k_k, shp, jnp.float32, -bound, bound)
        w_v = jax.random.uniform(k_v, shp, jnp.float32, -bound, bound)
        return {'x': x, 'w_q': w_q, 'w_k': w_k, 'w_v': w_v}
    _L0_attn_all = _L0_attn_setup()
    _L0_attn_in = {k: v for k, v in _L0_attn_all.items() if k in ('w_q', 'w_k', 'w_v')}
    del _L0_attn_all

    def _L0_ffn_setup():
        import jax, jax.numpy as jnp
        import numpy as np
        B, S, DIM = (4, 1024, 256)
        BASE_COUPLING = 0.1
        NUM_CYCLES = 3

        def _gelu(x):
            return jax.nn.gelu(x, approximate=False)

        def _coupling_net(h, w1, b1, w2, b2, w3, b3, w4, b4):
            h = _gelu(h @ w1 + b1)
            h = _gelu(h @ w2 + b2)
            h = _gelu(h @ w3 + b3)
            return jax.nn.sigmoid(h @ w4 + b4)

        def _global_net(h, w1, b1, w2, b2, w3, b3):
            h = _gelu(h @ w1 + b1)
            h = _gelu(h @ w2 + b2)
            return jax.nn.sigmoid(h @ w3 + b3)

        def _twist(x):
            o_r, o_i, p_r, p_i = jnp.split(x, 4, axis=-1)
            return jnp.concatenate([p_r, -p_i, -o_r, o_i], axis=-1)
        key = jax.random.key(seed)
        ks = jax.random.split(key, 9)
        d = DIM

        def w(k, fan_in, fan_out):
            return jax.random.normal(k, (fan_in, fan_out), dtype=jnp.float32) / np.sqrt(fan_in).astype(np.float32)
        inp = {'x': jax.random.normal(ks[0], (B, S, d), dtype=jnp.float32)}
        cn_dims = [(d, d), (d, d // 2), (d // 2, d // 4), (d // 4, 1)]
        for i, (a, b) in enumerate(cn_dims):
            inp[f'cn_w{i + 1}'] = w(ks[1 + i], a, b)
            inp[f'cn_b{i + 1}'] = jnp.zeros((b,), dtype=jnp.float32)
        gc_dims = [(d, d // 2), (d // 2, d // 4), (d // 4, 1)]
        for i, (a, b) in enumerate(gc_dims):
            inp[f'gc_w{i + 1}'] = w(ks[5 + i], a, b)
            inp[f'gc_b{i + 1}'] = jnp.zeros((b,), dtype=jnp.float32)
        inp['adaptive_range'] = jnp.full((1,), 0.2, dtype=jnp.float32)
        return inp
    _L0_ffn_all = _L0_ffn_setup()
    _L0_ffn_in = {k: v for k, v in _L0_ffn_all.items() if k in ('cn_w1', 'cn_b1', 'cn_w2', 'cn_b2', 'cn_w3', 'cn_b3', 'cn_w4', 'cn_b4', 'gc_w1', 'gc_b1', 'gc_w2', 'gc_b2', 'gc_w3', 'gc_b3', 'adaptive_range')}
    del _L0_ffn_all
    return {'x': x, 'mask_BS_i1_0': mask_BS_i1_0, 'L0_tok_token_W': _L0_tok_in['token_W'], 'L0_tok_pos_W': _L0_tok_in['pos_W'], 'L0_tok_type_W': _L0_tok_in['type_W'], 'L0_tok_ln_w': _L0_tok_in['ln_w'], 'L0_tok_ln_b': _L0_tok_in['ln_b'], 'L0_attn_w_q': _L0_attn_in['w_q'], 'L0_attn_w_k': _L0_attn_in['w_k'], 'L0_attn_w_v': _L0_attn_in['w_v'], 'L0_ffn_cn_w1': _L0_ffn_in['cn_w1'], 'L0_ffn_cn_b1': _L0_ffn_in['cn_b1'], 'L0_ffn_cn_w2': _L0_ffn_in['cn_w2'], 'L0_ffn_cn_b2': _L0_ffn_in['cn_b2'], 'L0_ffn_cn_w3': _L0_ffn_in['cn_w3'], 'L0_ffn_cn_b3': _L0_ffn_in['cn_b3'], 'L0_ffn_cn_w4': _L0_ffn_in['cn_w4'], 'L0_ffn_cn_b4': _L0_ffn_in['cn_b4'], 'L0_ffn_gc_w1': _L0_ffn_in['gc_w1'], 'L0_ffn_gc_b1': _L0_ffn_in['gc_b1'], 'L0_ffn_gc_w2': _L0_ffn_in['gc_w2'], 'L0_ffn_gc_b2': _L0_ffn_in['gc_b2'], 'L0_ffn_gc_w3': _L0_ffn_in['gc_w3'], 'L0_ffn_gc_b3': _L0_ffn_in['gc_b3'], 'L0_ffn_adaptive_range': _L0_ffn_in['adaptive_range']}

def reference(x, mask_BS_i1_0, L0_tok_token_W, L0_tok_pos_W, L0_tok_type_W, L0_tok_ln_w, L0_tok_ln_b, L0_attn_w_q, L0_attn_w_k, L0_attn_w_v, L0_ffn_cn_w1, L0_ffn_cn_b1, L0_ffn_cn_w2, L0_ffn_cn_b2, L0_ffn_cn_w3, L0_ffn_cn_b3, L0_ffn_cn_w4, L0_ffn_cn_b4, L0_ffn_gc_w1, L0_ffn_gc_b1, L0_ffn_gc_w2, L0_ffn_gc_b2, L0_ffn_gc_w3, L0_ffn_gc_b3, L0_ffn_adaptive_range):
    import jax
    import jax.numpy as jnp

    def _L0_tok_ref(input_ids, token_type_ids, token_W, pos_W, type_W, ln_w, ln_b):
        import jax, jax.numpy as jnp
        import numpy as np
        EPS = 1e-05
        S = input_ids.shape[-1]
        te = token_W[input_ids]
        tte = type_W[token_type_ids]
        pe = pos_W[:S][None, :, :]
        e = te + tte + pe
        mean = jax.lax.stop_gradient(jnp.mean(e, axis=-1, keepdims=True))
        var = jax.lax.stop_gradient(jnp.var(e, axis=-1, keepdims=True))
        normalized = (e - mean) / jnp.sqrt(var + EPS)
        return normalized * ln_w + ln_b

    def _L0_attn_ref(x, w_q, w_k, w_v):
        import jax, jax.numpy as jnp
        import numpy as np
        D_MODEL = 256
        N_HEADS = 16
        HEAD_D = D_MODEL // N_HEADS
        B, T = (4, 1024)
        ROPE_BASE = 10000.0

        def _rope(x):
            Bx, Tx, Dx = x.shape
            half = Dx // 2
            inv_freq = 1.0 / ROPE_BASE ** (jnp.arange(half, dtype=jnp.float32) / half)
            ang = jnp.arange(Tx, dtype=jnp.float32)[:, None] * inv_freq[None, :]
            cos, sin = (jnp.cos(ang), jnp.sin(ang))
            x1 = x[..., 0::2]
            x2 = x[..., 1::2]
            r1 = x1 * cos - x2 * sin
            r2 = x1 * sin + x2 * cos
            out = jnp.stack([r1, r2], axis=-1).reshape(Bx, Tx, Dx)
            return out
        Bx, Tx, Dx = x.shape
        d = Dx // N_HEADS
        xh = x.reshape(Bx, Tx, d, N_HEADS)
        q = jnp.einsum('btqh,qdh->btdh', xh, w_q).reshape(Bx, Tx, Dx)
        k = jnp.einsum('btkh,kdh->btdh', xh, w_k).reshape(Bx, Tx, Dx)
        v = jnp.einsum('btvh,vdh->btdh', xh, w_v).reshape(Bx, Tx, Dx)
        q = _rope(q)
        k = _rope(k)
        gamma = 1.0 / jnp.sqrt(jnp.float32(Dx))
        scores = jnp.einsum('bqd,bkd->bqk', q, k) * gamma
        causal = jnp.tril(jnp.ones((Tx, Tx), dtype=bool))
        scores = jnp.where(causal[None], scores, -jnp.inf)
        attn = jax.nn.softmax(scores, axis=-1)
        y = jnp.einsum('bqt,btd->bqd', attn, v)
        return y

    def _L0_ffn_ref(x, cn_w1, cn_b1, cn_w2, cn_b2, cn_w3, cn_b3, cn_w4, cn_b4, gc_w1, gc_b1, gc_w2, gc_b2, gc_w3, gc_b3, adaptive_range):
        import jax, jax.numpy as jnp
        import numpy as np
        B, S, DIM = (4, 1024, 256)
        BASE_COUPLING = 0.1
        NUM_CYCLES = 3

        def _gelu(x):
            return jax.nn.gelu(x, approximate=False)

        def _coupling_net(h, w1, b1, w2, b2, w3, b3, w4, b4):
            h = _gelu(h @ w1 + b1)
            h = _gelu(h @ w2 + b2)
            h = _gelu(h @ w3 + b3)
            return jax.nn.sigmoid(h @ w4 + b4)

        def _global_net(h, w1, b1, w2, b2, w3, b3):
            h = _gelu(h @ w1 + b1)
            h = _gelu(h @ w2 + b2)
            return jax.nn.sigmoid(h @ w3 + b3)

        def _twist(x):
            o_r, o_i, p_r, p_i = jnp.split(x, 4, axis=-1)
            return jnp.concatenate([p_r, -p_i, -o_r, o_i], axis=-1)
        global_context = x.mean(axis=1, keepdims=True)
        gf = _global_net(global_context, gc_w1, gc_b1, gc_w2, gc_b2, gc_w3, gc_b3)
        out = x
        for _ in range(NUM_CYCLES):
            tf = _coupling_net(out, cn_w1, cn_b1, cn_w2, cn_b2, cn_w3, cn_b3, cn_w4, cn_b4)
            combined = 0.7 * gf + 0.3 * tf
            coupling = BASE_COUPLING + adaptive_range * (combined - 0.5) * 2.0
            out = out + coupling * _twist(out)
        return out
    h = _L0_tok_ref(x, mask_BS_i1_0, L0_tok_token_W, L0_tok_pos_W, L0_tok_type_W, L0_tok_ln_w, L0_tok_ln_b)
    h = h + _L0_attn_ref(_layernorm(h, axis=-1), L0_attn_w_q, L0_attn_w_k, L0_attn_w_v)
    h = h + _L0_ffn_ref(_layernorm(h, axis=-1), L0_ffn_cn_w1, L0_ffn_cn_b1, L0_ffn_cn_w2, L0_ffn_cn_b2, L0_ffn_cn_w3, L0_ffn_cn_b3, L0_ffn_cn_w4, L0_ffn_cn_b4, L0_ffn_gc_w1, L0_ffn_gc_b1, L0_ffn_gc_w2, L0_ffn_gc_b2, L0_ffn_gc_w3, L0_ffn_gc_b3, L0_ffn_adaptive_range)
    return h

_drawn_inputs = setup_inputs


def setup_inputs(seed=0):
    import zlib

    import numpy as np

    out = dict(_drawn_inputs(seed))
    spreads = {'L0_tok_ln_w': (1.0, 0.2),
     'L0_tok_ln_b': (0.0, 0.1),
     'L0_ffn_cn_b1': (0.0, 2.0),
     'L0_ffn_cn_b2': (0.0, 2.0),
     'L0_ffn_cn_b3': (0.0, 2.0),
     'L0_ffn_gc_b1': (0.0, 0.8),
     'L0_ffn_gc_b2': (0.0, 0.8)}
    factors = {'L0_attn_w_q': 8.0,
     'L0_attn_w_k': 8.0,
     'L0_ffn_cn_w1': 6.94,
     'L0_ffn_cn_w2': 5.918,
     'L0_ffn_cn_w3': 7.518,
     'L0_ffn_cn_w4': 6.514,
     'L0_ffn_gc_w1': 8.0,
     'L0_ffn_gc_w2': 8.0,
     'L0_ffn_gc_w3': 6.698}
    for name, (base, spread) in spreads.items():
        noise = np.random.default_rng([zlib.crc32(name.encode()), seed]).standard_normal(out[name].shape)
        drawn = base * np.exp(spread * noise) if base else spread * noise
        out[name] = jnp.asarray(drawn.astype(out[name].dtype))
    for name, factor in factors.items():
        out[name] = (out[name] * factor).astype(out[name].dtype)
    return out
```

```python
from contextlib import ExitStack

import numpy as np

import concourse.bass as bass
from concourse import mybir

ALU = mybir.AluOpType
ACT = mybir.ActivationFunctionType
F32 = mybir.dt.float32
I32 = mybir.dt.int32
AX = mybir.AxisListType

P = 128
NB = 16
D = 256
H = 16
HD = D // H
PAIRS = NB // 2
GROUPS = NB // 4
NG = 4 * P
CYCLES = 3
EPS = 1e-5
BASE_COUPLING = 0.1
SCORE_SCALE = 1.0 / 16.0
MASKED = -1e30
FIRST_PAIRS = 3

C_IDENT, C_COS, C_SIN, C_MASK, C_HEAD, C_SIGN = 0, P, 2 * P, 3 * P, 4 * P, 4 * P + H // 2
C_END = C_SIGN + 1
E_POS, E_TYPE0, E_TYPE1, E_LNW, E_LNB = 0, D, 2 * D, 3 * D, 4 * D
F_W1, F_W2, F_W3 = 0, 2 * D, 2 * D + 2 * P
F_G1, F_G2 = F_W3 + 64, F_W3 + 64 + 2 * P
F_W4, F_G3 = F_G2 + 64, F_G2 + 65
F_B1, F_B2, F_B3, F_B4 = F_G3 + 1, F_G3 + 3, F_G3 + 4, F_G3 + 5
F_GB1, F_GB2, F_GB3, F_AR = F_B4 + 1, F_B4 + 2, F_B4 + 3, F_B4 + 4
F_END = F_AR + 1


def tower(nc, ids, emb, consts, attn_w, ffn_w, token_w, out):
    ctx = ExitStack()
    with ctx:
        def sb(name, shape, dt=F32):
            return ctx.enter_context(nc.sbuf_tensor(name, shape, dt))

        def sem(name):
            return ctx.enter_context(nc.semaphore(name))

        ids_sb = sb("ids_sb", [P, 2 * NB], I32)
        emb_sb = sb("emb_sb", [P, 5 * D])
        con = sb("con", [P, C_END])
        aw = sb("aw", [P, 6, HD])
        fw = sb("fw", [P, F_END])
        typef = sb("typef", [P, NB])
        pos0 = sb("pos0", [P, D])
        tdiff = sb("tdiff", [P, D])
        wqkv = sb("wqkv", [P, 6, HD, H // 2])
        w1t = sb("w1t", [P, 2, D])
        w4w = sb("w4w", [64, P])
        g3w = sb("g3w", [64, P])
        half_b4 = sb("half_b4", [P, 1])
        half_gb3 = sb("half_gb3", [P, 1])
        ar03 = sb("ar03", [P, 1])
        ar07 = sb("ar07", [P, 1])
        neg_half = sb("neg_half", [P, 2])
        ones = sb("ones", [64, P])

        h = sb("h", [P, NB, D])
        x2m = sb("x2m", [P, NB])
        x2r = sb("x2r", [P, NB])

        st_e = sb("st_e", [P, 2, 6]); mv_e = sb("mv_e", [P, 2, 2]); ve_e = sb("ve_e", [P, 2]); rs_e = sb("rs_e", [P, 2])
        st_a = sb("st_a", [P, 2, 6]); mv_a = sb("mv_a", [P, 2, 2]); ve_a = sb("ve_a", [P, 2]); rs_a = sb("rs_a", [P, 2])
        st_f = sb("st_f", [P, 2, 6]); mv_f = sb("mv_f", [P, 2, 2]); ve_f = sb("ve_f", [P, 2]); rs_f = sb("rs_f", [P, 2])
        xn = sb("xn", [P, 2, 2, P])
        xT = sb("xT", [P, 2, 2, P])
        tcos = sb("tcos", [P, 2, 2, 2, P])
        tsin = sb("tsin", [P, 2, 2, 2, P])
        rot = sb("rot", [P, 2, 2, 2, P])
        v_sb = sb("v_sb", [P, 2, D])
        sc = sb("sc", [P, 2, P])
        nmax = sb("nmax", [P, 2])
        prob = sb("prob", [P, 2, P])
        psum_row = sb("psum_row", [P, 2])
        rinv = sb("rinv", [P, 2])
        probT = sb("probT", [P, 2, P])
        x2 = sb("x2", [P, 2, D])
        x2T = sb("x2T", [P, 2, 2, P])
        gsum = sb("gsum", [P, 2, NB])

        pre = sb("pre", [P, 2, NB * P])
        tw = sb("tw", [P, 2, NB * P])
        a1 = sb("a1", [P, 2, 2, NG])
        a2 = sb("a2", [P, 2, NG])
        a3 = sb("a3", [64, 2, NG])
        tz = sb("tz", [P, 2, NG])
        cpl = sb("cpl", [P, 2, 4, P])
        up = sb("up", [P, 2, NG])
        ut = sb("ut", [P, 2, NG])
        g1 = sb("g1", [P, NB]); g2 = sb("g2", [64, NB]); tg = sb("tg", [P, NB]); base = sb("base", [P, NB])
        tcol = sb("tcol", [P, CYCLES, NB])
        ccol = sb("ccol", [P, CYCLES, NB])
        cw = sb("cw", [P, 8, NB])
        xf = sb("xf", [P, 4, D])

        banks = [ctx.enter_context(nc.psum_tensor(f"bank{i}", [P, 512], F32)) for i in range(8)]
        tr_ps = banks[0][:, :].rearrange("p (j a t) -> p j a t", j=2, a=2)
        q_ps = banks[1][:, :].rearrange("p (a t) -> p a t", a=2)
        k_ps = banks[2][:, :].rearrange("p (a t) -> p a t", a=2)
        v_ps = banks[3][:, :].rearrange("p (j a i) -> p j a i", j=2, a=2)
        s_ps = banks[4][:, 0:2 * P].rearrange("p (j t) -> p j t", j=2)
        pt_ps = banks[4][:, 2 * P:4 * P].rearrange("p (j t) -> p j t", j=2)
        y_ps = banks[6][:, :].rearrange("p (j d) -> p j d", j=2)
        pre_ps = banks[5][:, :].rearrange("p (m t) -> p m t", m=2)
        tw_ps = banks[7][:, :].rearrange("p (m t) -> p m t", m=2)

        ident = con[:, C_IDENT:C_IDENT + P]
        cos_b = con[:, C_COS:C_COS + P].unsqueeze(1).broadcast_to([P, 4, P])
        sin_b = con[:, C_SIN:C_SIN + P].unsqueeze(1).broadcast_to([P, 4, P])
        mask = con[:, C_MASK:C_MASK + P]
        lnw = emb_sb[:, E_LNW:E_LNW + D]
        lnb = emb_sb[:, E_LNB:E_LNB + D]
        w1 = fw[:, F_W1:F_W1 + 2 * D].rearrange("p (k n) -> p k n", k=2)
        w2 = fw[:, F_W2:F_W2 + 2 * P].rearrange("p (k n) -> p k n", k=2)
        w3 = fw[:, F_W3:F_W3 + 64]
        gw1 = fw[:, F_G1:F_G1 + 2 * P].rearrange("p (k n) -> p k n", k=2)
        gw2 = fw[:, F_G2:F_G2 + 64]

        def w_attn(m, par):
            return wqkv[:, 2 * m + par, :, :].rearrange("p d i -> p (d i)")

        ids_in = sem("ids_in"); emb_in = sem("emb_in"); con_in = sem("con_in")
        aw_in = sem("aw_in"); fw_in = sem("fw_in"); out_done = sem("out_done")
        rows_in = [sem(f"rows_in{b}") for b in range(2 * FIRST_PAIRS)]
        rest_in = sem("rest_in")
        prep = sem("prep")
        prefilled = sem("prefilled")
        wqkv_ready = sem("wqkv_ready"); ffn_ready = sem("ffn_ready"); half_ready = sem("half_ready")
        e_stats = sem("e_stats"); e_mv = sem("e_mv"); e_var = sem("e_var"); e_rstd = sem("e_rstd")
        e_cent = sem("e_cent"); h0_ready = sem("h0_ready")
        a_stats = sem("a_stats"); a_mv = sem("a_mv"); a_var = sem("a_var"); a_rstd = sem("a_rstd")
        xn_ready = sem("xn_ready")
        xn_turned = sem("xn_turned"); xT_ready = sem("xT_ready")
        q_ready = sem("q_ready"); k_ready = sem("k_ready")
        q_parts = sem("q_parts"); k_parts = sem("k_parts"); rot_ready = sem("rot_ready")
        scored = sem("scored"); sc_ready = sem("sc_ready"); prob_ready = sem("prob_ready")
        prob_turned = sem("prob_turned"); probT_ready = sem("probT_ready")
        v_made = sem("v_made"); v_ready = sem("v_ready"); y_made = sem("y_made")
        rinv_ready = sem("rinv_ready"); h1_ready = sem("h1_ready")
        f_stats = sem("f_stats"); f_mv = sem("f_mv"); f_var = sem("f_var"); f_rstd = sem("f_rstd")
        x2_ready = sem("x2_ready"); x2_turned = sem("x2_turned"); x2T_ready = sem("x2T_ready")
        mean_ready = sem("mean_ready"); x2T_used = sem("x2T_used")
        pre_made = sem("pre_made"); tw_made = sem("tw_made")
        pre_out = sem("pre_out"); tw_out = sem("tw_out")
        g_mm = sem("g_mm"); g_act = sem("g_act"); base_ready = sem("base_ready")
        a1_ready = sem("a1_ready"); l2_made = sem("l2_made"); a2_ready = sem("a2_ready")
        l3_made = sem("l3_made"); a3_ready = sem("a3_ready"); l4_made = sem("l4_made")
        zcol_made = sem("zcol_made")
        tz_ready = sem("tz_ready"); tcol_ready = sem("tcol_ready")
        cpl_ready = sem("cpl_ready"); prod_ready = sem("prod_ready"); pre_new = sem("pre_new")
        tw_new = sem("tw_new"); small = sem("small"); xf_ready = sem("xf_ready")
        mixed = sem("mixed"); h_out = sem("h_out")

        def at_least(eng, s, v):
            if not (isinstance(v, int) and v <= 0):
                eng.wait_ge(s, v)

        def wait_alone(eng, s, v):
            v = v if isinstance(v, int) else eng.to_reg(v)
            eng.wait_ge(con_in, 16)
            eng.wait_ge(s, v)

        def phases(eng, body):
            body(-1, "E")
            body(0, "EX")
            body(1, "EXA")
            with eng.Fori(2, PAIRS - 1) as i:
                body(i, "EXAF")
            body(PAIRS - 1, "XAF")
            body(PAIRS, "AF")
            body(PAIRS + 1, "F")

        block = ctx.enter_context(nc.Block())

        @block.sync
        def _(sp):
            sp.dma_start(ids_sb[:, :], ids).then_inc(ids_in, 16)
            sp.dma_start(emb_sb[:, :], emb).then_inc(emb_in, 16)
            sp.dma_start(con[:, :], consts).then_inc(con_in, 16)
            sp.dma_start(aw[:, :, :], attn_w).then_inc(aw_in, 16)
            sp.dma_start(fw[:, :], ffn_w).then_inc(fw_in, 16)
            for g in range(GROUPS):
                sp.wait_ge(h_out, 4 * (g + 1))
                sp.dma_start(out[4 * g:4 * g + 4].rearrange("b t d -> t b d"),
                             h[:, 4 * g:4 * g + 4, :]).then_inc(out_done, 16)
            sp.wait_ge(out_done, 16 * GROUPS)

        @block.gpsimd
        def _(pool):
            def gather(b):
                pool.wait_ge(prefilled, b + 1)
                pool.indirect_dma_start(
                    out=h[:, b, :], out_offset=None, in_=token_w,
                    in_offset=bass.IndirectOffsetOnAxis(ap=ids_sb[:, b:b + 1], axis=0),
                    compute_op=ALU.add,
                ).then_inc(rows_in[b] if b < 2 * FIRST_PAIRS else rest_in, 16)

            pool.wait_ge(ids_in, 16)
            for b in range(4):
                gather(b)
            pool.wait_ge(prep, 5)

            def body(i, what):
                if "E" in what:
                    pool.wait_ge(e_var, i + 2)
                    at_least(pool, h0_ready, 2 * (i + 1))
                    pool.tensor_tensor(rs_e[:, :], ve_e[:, :], neg_half[:, :], ALU.pow).then_inc(e_rstd, 1)
                if "X" in what:
                    pool.wait_ge(q_parts, i + 1)
                    at_least(pool, scored, i)
                    pool.tensor_tensor(rot[:, 0, 0], tcos[:, 0, 0], tsin[:, 0, 1], ALU.subtract).then_inc(rot_ready, 1)
                    pool.tensor_tensor(rot[:, 0, 1], tcos[:, 0, 1], tsin[:, 0, 0], ALU.add).then_inc(rot_ready, 1)
                if "E" in what:
                    pool.wait_ge(a_var, i + 2)
                    at_least(pool, xn_ready, 2 * (i + 1))
                    pool.tensor_tensor(rs_a[:, :], ve_a[:, :], neg_half[:, :], ALU.pow).then_inc(a_rstd, 1)
                if "X" in what:
                    pool.wait_ge(k_parts, i + 1)
                    pool.tensor_tensor(rot[:, 1, 0], tcos[:, 1, 0], tsin[:, 1, 1], ALU.subtract).then_inc(rot_ready, 1)
                    pool.tensor_tensor(rot[:, 1, 1], tcos[:, 1, 1], tsin[:, 1, 0], ALU.add).then_inc(rot_ready, 1)
                if "A" in what:
                    pool.wait_ge(f_var, i)
                    at_least(pool, x2_ready, 2 * (i - 1))
                    pool.tensor_tensor(rs_f[:, :], ve_f[:, :], neg_half[:, :], ALU.pow).then_inc(f_rstd, 1)
                if isinstance(i, int) and i in (-1, 0):
                    for b in ((4, 5, 6, 7, 8, 9) if i < 0 else range(10, NB)):
                        gather(b)

            phases(pool, body)

        @block.tensor
        def _(pe):
            pe.wait_ge(con_in, 16)

            def body(i, what):
                if "A" in what:
                    pe.wait_ge(rot_ready, 4 * i)
                    at_least(pe, probT_ready, i - 1)
                    for j in range(2):
                        for par in range(2):
                            mm = pe.matmul(s_ps[:, j, :], rot[:, 0, par, j, :], rot[:, 1, par, j, :],
                                           start=(par == 0), stop=(par == 1))
                    mm.then_inc(scored, 1)
                if "X" in what:
                    pe.wait_ge(xn_ready, 2 * (i + 1))
                    at_least(pe, x2T_ready, i - 2)
                    for j in range(2):
                        for par in range(2):
                            mm = pe.transpose(tr_ps[:, j, par, :], xn[:, j, par, :], ident)
                    mm.then_inc(xn_turned, 1)
                if "A" in what:
                    pe.wait_ge(prob_ready, 2 * i)
                    for j in range(2):
                        mm = pe.transpose(pt_ps[:, j, :], prob[:, j, :], ident)
                    mm.then_inc(prob_turned, 1)
                if "X" in what:
                    pe.wait_ge(xT_ready, i + 1)
                    if isinstance(i, int) and i == 0:
                        pe.wait_ge(wqkv_ready, 1)
                    for m, (ps, used, made) in enumerate(((q_ps, q_parts, q_ready), (k_ps, k_parts, k_ready))):
                        at_least(pe, used, i)
                        for par in range(2):
                            mm = pe.matmul(ps[:, par, :], w_attn(m, par),
                                           xT[:, par, :, :].rearrange("p j t -> p (j t)"),
                                           start=True, stop=True)
                        mm.then_inc(made, 1)
                if "A" in what:
                    pe.wait_ge(probT_ready, i)
                    pe.wait_ge(v_ready, i)
                    at_least(pe, h1_ready, 2 * (i - 1))
                    for j in range(2):
                        mm = pe.matmul(y_ps[:, j, :], probT[:, j, :], v_sb[:, j, :], start=True, stop=True)
                    mm.then_inc(y_made, 1)
                if "X" in what:
                    at_least(pe, v_ready, i)
                    for j in range(2):
                        for par in range(2):
                            mm = pe.matmul(v_ps[:, j, par, :], xT[:, par, j, :], w_attn(2, par),
                                           start=True, stop=True)
                    mm.then_inc(v_made, 1)
                if "F" in what:
                    pe.wait_ge(x2_ready, 2 * (i - 1))
                    if "X" in what:
                        pe.wait_ge(xT_ready, i + 1)
                    else:
                        at_least(pe, x2T_ready, i - 2)
                    for j in range(2):
                        for a in range(2):
                            mm = pe.transpose(tr_ps[:, j, a, :], x2[:, j, a * P:(a + 1) * P], ident)
                    mm.then_inc(x2_turned, 1)
                    pe.wait_ge(x2T_ready, i - 1)
                    if isinstance(i, int) and i == 2 or not isinstance(i, int):
                        pe.wait_ge(ffn_ready, 4)
                    for w, ps, left, made in ((w1, pre_ps, pre_out, pre_made), (w1t, tw_ps, tw_out, tw_made)):
                        at_least(pe, left, i - 2)
                        for m in range(2):
                            for k in range(2):
                                mm = pe.matmul(ps[:, m, :], w[:, k, m * P:(m + 1) * P],
                                               x2T[:, k, :, :].rearrange("p j t -> p (j t)"),
                                               start=(k == 0), stop=(k == 1))
                        mm.then_inc(made, 1)

            phases(pe, body)

            pe.wait_ge(mean_ready, PAIRS)
            for k in range(2):
                mm = pe.matmul(banks[1][:, 0:NB], gw1[:, k, :], gsum[:, k, :], start=(k == 0), stop=(k == 1))
            mm.then_inc(g_mm, 1)
            pe.wait_ge(g_act, 1)
            pe.matmul(banks[2][0:64, 0:NB], gw2, g1[:, :], start=True, stop=True).then_inc(g_mm, 1)
            pe.wait_ge(g_act, 2)
            pe.matmul(banks[3][:, 0:NB], g3w[:, :], g2[:, :], start=True, stop=True).then_inc(g_mm, 1)
            pe.wait_ge(g_act, 3)

            items = CYCLES * GROUPS
            for n in range(items + 2):
                if n < items:
                    pe.wait_ge(a1_ready, n + 1)
                    at_least(pe, a2_ready, n - 1)
                    for k in range(2):
                        mm = pe.matmul(banks[n % 2][:, :], w2[:, k, :], a1[:, n % 2, k, :],
                                       start=(k == 0), stop=(k == 1))
                    mm.then_inc(l2_made, 1)
                if 1 <= n <= items:
                    pe.wait_ge(a2_ready, n)
                    at_least(pe, a3_ready, n - 2)
                    pe.matmul(banks[2 + (n - 1) % 2][0:64, :], w3, a2[:, (n - 1) % 2, :],
                              start=True, stop=True).then_inc(l3_made, 1)
                if n >= 2:
                    m = n - 2
                    pe.wait_ge(a3_ready, m + 1)
                    if m < items - GROUPS:
                        at_least(pe, tz_ready, m - 1)
                        pe.matmul(banks[4 + m % 2][:, :], w4w[:, :], a3[:, m % 2, :],
                                  start=True, stop=True).then_inc(l4_made, 1)
                    at_least(pe, tcol_ready, m - 1)
                    for j in range(4):
                        mm = pe.matmul(banks[6 + m % 2][:, j:j + 1], a3[:, m % 2, j * P:(j + 1) * P],
                                       fw[0:64, F_W4:F_W4 + 1], start=True, stop=True)
                    mm.then_inc(zcol_made, 1)

        @block.scalar
        def _(act):
            def body(i, what):
                if "X" in what:
                    act.wait_ge(xn_turned, i + 1)
                    at_least(act, v_made, i)
                    act.activation(xT[:, :, :, :], tr_ps.rearrange("p j a t -> p a j t"),
                                   ACT.Copy).then_inc(xT_ready, 1)
                if "A" in what:
                    for j in range(2):
                        act.wait_ge(sc_ready, 2 * (i - 1) + j + 1)
                        if j == 0:
                            at_least(act, prob_turned, i - 1)
                            at_least(act, rinv_ready, i - 1)
                        act.activation(prob[:, j, :], sc[:, j, :], ACT.Exp, bias=nmax[:, j:j + 1], scale=-1.0,
                                       accum_out=psum_row[:, j:j + 1]).then_inc(prob_ready, 1)
                    act.wait_ge(prob_turned, i)
                    at_least(act, y_made, i - 1)
                    act.activation(probT[:, :, :], pt_ps, ACT.Copy).then_inc(probT_ready, 1)
                if "X" in what:
                    act.wait_ge(v_made, i + 1)
                    at_least(act, y_made, i)
                    act.activation(v_sb[:, :, :].rearrange("p j (i a) -> p j a i", a=2), v_ps,
                                   ACT.Copy).then_inc(v_ready, 1)
                if "F" in what:
                    act.wait_ge(x2_turned, i - 1)
                    at_least(act, tw_made, i - 2)
                    at_least(act, mean_ready, i - 2)
                    act.activation(x2T[:, :, :, :], tr_ps.rearrange("p j a t -> p a j t"),
                                   ACT.Copy).then_inc(x2T_ready, 1)
                    act.wait_ge(pre_made, i - 1)
                    act.activation(pre[:, :, bass.ds((i - 2) * (2 * P), 2 * P)], pre_ps, ACT.Copy).then_inc(pre_out, 1)
                    act.wait_ge(tw_made, i - 1)
                    act.activation(tw[:, :, bass.ds((i - 2) * (2 * P), 2 * P)], tw_ps, ACT.Copy).then_inc(tw_out, 1)

            phases(act, body)

            act.wait_ge(fw_in, 16)
            act.wait_ge(half_ready, 2)
            act.wait_ge(g_mm, 1)
            act.activation(g1[:, :], banks[1][:, 0:NB], ACT.Gelu, bias=fw[:, F_GB1:F_GB1 + 1],
                           scale=1.0 / P).then_inc(g_act, 1)
            act.wait_ge(g_mm, 2)
            act.activation(g2[:, :], banks[2][0:64, 0:NB], ACT.Gelu,
                           bias=fw[0:64, F_GB2:F_GB2 + 1]).then_inc(g_act, 1)
            act.wait_ge(g_mm, 3)
            act.activation(tg[:, :], banks[3][:, 0:NB], ACT.Tanh, bias=half_gb3[:, :],
                           scale=0.5).then_inc(g_act, 1)

            items = CYCLES * GROUPS

            def first(n):
                g = n % GROUPS
                if n < GROUPS:
                    act.wait_ge(pre_out, 2 * (g + 1))
                else:
                    act.wait_ge(pre_new, n - GROUPS + 1)
                at_least(act, l2_made, n - 1)
                for k in range(2):
                    ins = act.activation(a1[:, n % 2, k, :], pre[:, k, g * NG:(g + 1) * NG], ACT.Gelu,
                                         bias=fw[:, F_B1 + k:F_B1 + k + 1])
                ins.then_inc(a1_ready, 1)

            def last(m):
                g = m % GROUPS
                if m < items - GROUPS:
                    act.wait_ge(l4_made, m + 1)
                    at_least(act, cpl_ready, m - 1)
                    act.activation(tz[:, m % 2, :], banks[4 + m % 2][:, :], ACT.Tanh, bias=half_b4[:, :],
                                   scale=0.5).then_inc(tz_ready, 1)
                act.wait_ge(zcol_made, m + 1)
                act.activation(tcol[:, m // GROUPS, 4 * g:4 * g + 4], banks[6 + m % 2][:, 0:4], ACT.Tanh,
                               bias=half_b4[:, :], scale=0.5).then_inc(tcol_ready, 1)

            first(0)
            for n in range(items + 2):
                if n + 1 < GROUPS:
                    first(n + 1)
                if n < items:
                    act.wait_ge(l2_made, n + 1)
                    at_least(act, l3_made, n - 1)
                    act.activation(a2[:, n % 2, :], banks[n % 2][:, :], ACT.Gelu,
                                   bias=fw[:, F_B2:F_B2 + 1]).then_inc(a2_ready, 1)
                if 1 <= n <= items:
                    act.wait_ge(l3_made, n)
                    at_least(act, zcol_made, n - 2)
                    act.activation(a3[:, (n - 1) % 2, :], banks[2 + (n - 1) % 2][0:64, :], ACT.Gelu,
                                   bias=fw[0:64, F_B3:F_B3 + 1]).then_inc(a3_ready, 1)
                if n >= 2:
                    last(n - 2)
                if GROUPS <= n + 1 < items:
                    first(n + 1)
                if n >= items - GROUPS + 2:
                    normalise = n - (items - GROUPS + 2)
                    g = normalise
                    at_least(act, h_out, 4 * g)
                    for j in range(4):
                        b = 4 * g + j
                        ins = act.activation(xf[:, j, :], h[:, b, :], ACT.Identity, bias=x2m[:, b:b + 1],
                                             scale=x2r[:, b:b + 1])
                    ins.then_inc(xf_ready, 1)

        @block.vector
        def _(dve):
            dve.memset(neg_half[:, :], -0.5).then_inc(prep, 1)
            dve.memset(ones[:, :], 1.0).then_inc(prep, 1)
            dve.wait_ge(ids_in, 16)
            dve.tensor_copy(typef[:, :], ids_sb[:, NB:2 * NB]).then_inc(prep, 1)
            dve.wait_ge(emb_in, 16)
            dve.tensor_tensor(pos0[:, :], emb_sb[:, E_POS:E_POS + D], emb_sb[:, E_TYPE0:E_TYPE0 + D],
                              ALU.add).then_inc(prep, 1)
            dve.tensor_tensor(tdiff[:, :], emb_sb[:, E_TYPE1:E_TYPE1 + D], emb_sb[:, E_TYPE0:E_TYPE0 + D],
                              ALU.subtract).then_inc(prep, 1)
            dve.wait_ge(prep, 5)
            for b in range(NB):
                dve.scalar_tensor_tensor(out=h[:, b, :], in0=tdiff[:, :], scalar=typef[:, b:b + 1],
                                         in1=pos0[:, :], op0=ALU.mult, op1=ALU.add).then_inc(prefilled, 1)
            dve.wait_ge(con_in, 16)
            dve.wait_ge(aw_in, 16)
            head = con[:, C_HEAD:C_HEAD + H // 2]
            dve.tensor_tensor(wqkv[:, :, :, :].rearrange("p m d i -> p (m d) i"),
                              aw[:, :, :].rearrange("p m d -> p (m d)").unsqueeze(2).broadcast_to([P, 6 * HD, H // 2]),
                              head.unsqueeze(1).broadcast_to([P, 6 * HD, H // 2]),
                              ALU.mult).then_inc(wqkv_ready, 1)
            dve.wait_ge(fw_in, 16)
            sign = con[:, C_SIGN:C_SIGN + 1]
            dve.tensor_scalar(w1t[:, 0, :], w1[:, 1, :], sign, None, ALU.mult).then_inc(ffn_ready, 1)
            dve.tensor_scalar(w1t[:, 1, :], w1[:, 0, :], sign, -1.0, ALU.mult, ALU.mult).then_inc(ffn_ready, 1)
            dve.tensor_scalar(w4w[:, :], ones[:, :], fw[0:64, F_W4:F_W4 + 1], None, ALU.mult).then_inc(ffn_ready, 1)
            dve.tensor_scalar(g3w[:, :], ones[:, :], fw[0:64, F_G3:F_G3 + 1], None, ALU.mult).then_inc(ffn_ready, 1)
            dve.tensor_scalar(half_b4[:, :], fw[:, F_B4:F_B4 + 1], 0.5, None, ALU.mult).then_inc(half_ready, 1)
            dve.tensor_scalar(half_gb3[:, :], fw[:, F_GB3:F_GB3 + 1], 0.5, None, ALU.mult).then_inc(half_ready, 1)
            dve.tensor_scalar(ar03[:, :], fw[:, F_AR:F_AR + 1], 0.3, None, ALU.mult).then_inc(prep, 1)
            dve.tensor_scalar(ar07[:, :], fw[:, F_AR:F_AR + 1], 0.7, None, ALU.mult).then_inc(prep, 1)

            def hrow(b):
                return h[:, bass.ds(b, 1), :].rearrange("p o d -> p (o d)")

            def layernorm_stats(rows, st, mv, ve, stats, mvs, var, done):
                for j in range(2):
                    dve.bn_stats(st[:, j, :], rows(j)).then_inc(stats, 1)
                for j in range(2):
                    wait_alone(dve, stats, 2 * done + j + 1)
                    dve.bn_aggr(mv[:, j, :], st[:, j, :]).then_inc(mvs, 1)
                dve.wait_ge(mvs, 2 * done + 2)
                dve.tensor_scalar(ve[:, :], mv[:, :, 1], EPS, None, ALU.add).then_inc(var, 1)

            def body(i, what):
                if "A" in what:
                    if not (isinstance(i, int) and i == 1):
                        wait_alone(dve, prob_ready, 2 * (i - 1))
                    wait_alone(dve, scored, i)
                    for j in range(2):
                        dve.tensor_tensor_reduce(sc[:, j, :], s_ps[:, j, :], mask, -SCORE_SCALE, 3e38,
                                                 ALU.add, ALU.min, nmax[:, j:j + 1]).then_inc(sc_ready, 1)
                if "E" in what:
                    if isinstance(i, int):
                        for j in range(2):
                            dve.wait_ge(rows_in[2 * (i + 1) + j], 16)
                        if i == FIRST_PAIRS - 2:
                            dve.wait_ge(rest_in, 16 * (NB - 2 * FIRST_PAIRS))
                    rows = [hrow(2 * i + 2), hrow(2 * i + 3)]
                    layernorm_stats(lambda j: rows[j], st_e, mv_e, ve_e, e_stats, e_mv, e_var, i + 1)
                    for j in range(2):
                        dve.scalar_tensor_tensor(out=rows[j], in0=rows[j], scalar=mv_e[:, j, 0:1], in1=lnw,
                                                 op0=ALU.subtract, op1=ALU.mult).then_inc(e_cent, 1)
                if "X" in what:
                    dve.wait_ge(q_ready, i + 1)
                    at_least(dve, rot_ready, 4 * i)
                    q4 = banks[1][:, :].rearrange("p (c t) -> p c t", c=4)
                    dve.tensor_tensor(tcos[:, 0].rearrange("p a j t -> p (a j) t"), q4, cos_b, ALU.mult)
                    dve.tensor_tensor(tsin[:, 0].rearrange("p a j t -> p (a j) t"), q4, sin_b,
                                      ALU.mult).then_inc(q_parts, 1)
                if "E" in what:
                    dve.wait_ge(e_rstd, i + 2)
                    dve.wait_ge(e_cent, 2 * (i + 2))
                    for j in range(2):
                        dve.scalar_tensor_tensor(out=rows[j], in0=rows[j], scalar=rs_e[:, j:j + 1], in1=lnb,
                                                 op0=ALU.mult, op1=ALU.add).then_inc(h0_ready, 1)
                    wait_alone(dve, h0_ready, 2 * (i + 2))
                    layernorm_stats(lambda j: rows[j], st_a, mv_a, ve_a, a_stats, a_mv, a_var, i + 1)
                if "X" in what:
                    dve.wait_ge(k_ready, i + 1)
                    k4 = banks[2][:, :].rearrange("p (c t) -> p c t", c=4)
                    dve.tensor_tensor(tcos[:, 1].rearrange("p a j t -> p (a j) t"), k4, cos_b, ALU.mult)
                    dve.tensor_tensor(tsin[:, 1].rearrange("p a j t -> p (a j) t"), k4, sin_b,
                                      ALU.mult).then_inc(k_parts, 1)
                if "E" in what:
                    dve.wait_ge(a_rstd, i + 2)
                    at_least(dve, xn_turned, i + 1)
                    for j in range(2):
                        dve.tensor_scalar(xn[:, j, :, :], rows[j].rearrange("p (i a) -> p a i", a=2),
                                          mv_a[:, j, 0:1], rs_a[:, j:j + 1], ALU.subtract,
                                          ALU.mult).then_inc(xn_ready, 1)
                if "A" in what:
                    dve.wait_ge(prob_ready, 2 * i)
                    dve.reciprocal(rinv[:, :], psum_row[:, :]).then_inc(rinv_ready, 1)
                    dve.wait_ge(rinv_ready, i)
                    dve.wait_ge(y_made, i)
                    mine = [hrow(2 * i - 2), hrow(2 * i - 1)]
                    for j in range(2):
                        dve.scalar_tensor_tensor(out=mine[j], in0=y_ps[:, j, :], scalar=rinv[:, j:j + 1],
                                                 in1=mine[j], op0=ALU.mult, op1=ALU.add).then_inc(h1_ready, 1)
                    wait_alone(dve, h1_ready, 2 * i)
                    layernorm_stats(lambda j: mine[j], st_f, mv_f, ve_f, f_stats, f_mv, f_var, i - 1)
                if "F" in what:
                    dve.wait_ge(x2T_ready, i - 1)
                    dve.tensor_reduce(gsum[:, :, bass.ds(2 * i - 4, 2)], x2T[:, :, :, :], AX.X,
                                      ALU.add).then_inc(mean_ready, 1)
                if "A" in what:
                    dve.wait_ge(f_rstd, i)
                    if "F" in what:
                        dve.wait_ge(x2_turned, i - 1)
                    for j in range(2):
                        dve.tensor_scalar(x2[:, j, :], mine[j], mv_f[:, j, 0:1], rs_f[:, j:j + 1],
                                          ALU.subtract, ALU.mult).then_inc(x2_ready, 1)
                    dve.tensor_copy(x2r[:, bass.ds(2 * i - 2, 2)], rs_f[:, :])
                    dve.scalar_tensor_tensor(out=x2m[:, bass.ds(2 * i - 2, 2)], in0=mv_f[:, :, 0], scalar=-1.0,
                                             in1=rs_f[:, :], op0=ALU.mult, op1=ALU.mult).then_inc(small, 1)

            phases(dve, body)

            dve.wait_ge(g_act, 3)
            dve.wait_ge(prep, 7)
            dve.tensor_scalar(base[:, :], tg[:, :], ar07[:, :], BASE_COUPLING, ALU.mult,
                              ALU.add).then_inc(base_ready, 1)
            dve.wait_ge(base_ready, 1)
            updates = (CYCLES - 1) * GROUPS
            for n in range(updates):
                g, s = n % GROUPS, n % 2
                cols = slice(g * NG, (g + 1) * NG)
                full = n < GROUPS
                dve.wait_ge(tz_ready, n + 1)
                for j in range(4):
                    ins = dve.tensor_scalar(cpl[:, s, j, :], tz[:, s, j * P:(j + 1) * P], ar03[:, :],
                                            base[:, 4 * g + j:4 * g + j + 1], ALU.mult, ALU.add)
                ins.then_inc(cpl_ready, 1)
                dve.wait_ge(cpl_ready, n + 1)
                c = cpl[:, s].rearrange("p j t -> p (j t)").unsqueeze(1).broadcast_to([P, 2, NG])
                if full:
                    dve.wait_ge(tw_out, 2 * (g + 1))
                at_least(dve, pre_new, n)
                at_least(dve, tw_new, min(n, GROUPS))
                ins = dve.tensor_tensor(up[:, :, :], tw[:, :, cols], c, ALU.mult)
                ins.then_inc(prod_ready, 1)
                if full:
                    dve.tensor_tensor(ut[:, :, :], pre[:, :, cols], c, ALU.mult).then_inc(prod_ready, 1)
                dve.wait_ge(prod_ready, 2 * (n + 1) if full else GROUPS + n + 1)
                dve.wait_ge(a1_ready, n + 1)
                dve.tensor_tensor(pre[:, :, cols], pre[:, :, cols], up[:, :, :], ALU.add).then_inc(pre_new, 1)
                if full:
                    dve.tensor_tensor(tw[:, :, cols], tw[:, :, cols], ut[:, :, :], ALU.subtract).then_inc(tw_new, 1)

            steps = [PAIRS]

            def step(ins):
                ins.then_inc(small, 1)
                steps[0] += 1
                dve.wait_ge(small, steps[0])

            for g in range(GROUPS):
                cols = slice(4 * g, 4 * g + 4)
                dve.wait_ge(tcol_ready, updates + g + 1)
                step(dve.scalar_tensor_tensor(out=ccol[:, :, cols], in0=tcol[:, :, cols], scalar=ar03[:, :],
                                              in1=base[:, cols].unsqueeze(1).broadcast_to([P, CYCLES, 4]),
                                              op0=ALU.mult, op1=ALU.add))
                c1, c2, c3 = (ccol[:, k, cols] for k in range(CYCLES))
                c12, alpha2, beta2, c3b, c3a, alpha, beta, nbeta = (cw[:, k, cols] for k in range(8))
                step(dve.tensor_tensor(c12, c1, c2, ALU.mult))
                dve.tensor_scalar(alpha2, c12, -1.0, 1.0, ALU.mult, ALU.add).then_inc(small, 1)
                steps[0] += 1
                step(dve.tensor_tensor(beta2, c1, c2, ALU.add))
                dve.tensor_tensor(c3b, c3, beta2, ALU.mult).then_inc(small, 1)
                steps[0] += 1
                step(dve.tensor_tensor(c3a, c3, alpha2, ALU.mult))
                dve.tensor_tensor(alpha, alpha2, c3b, ALU.subtract).then_inc(small, 1)
                steps[0] += 1
                step(dve.tensor_tensor(beta, beta2, c3a, ALU.add))
                step(dve.tensor_scalar(nbeta, beta, -1.0, None, ALU.mult))
                dve.wait_ge(xf_ready, g + 1)
                for j in range(4):
                    b = 4 * g + j
                    dve.scalar_tensor_tensor(out=h[:, b, :], in0=xf[:, j, :], scalar=cw[:, 5, b:b + 1],
                                             in1=h[:, b, :], op0=ALU.mult, op1=ALU.add).then_inc(mixed, 1)
                for j in range(4):
                    b = 4 * g + j
                    dve.wait_ge(mixed, 4 * g + j + 1)
                    for o, i, col in ((0, 2, 6), (1, 3, 7), (2, 0, 7), (3, 1, 6)):
                        dst = h[:, b, o * 64:(o + 1) * 64]
                        ins = dve.scalar_tensor_tensor(out=dst, in0=xf[:, j, i * 64:(i + 1) * 64],
                                                       scalar=cw[:, col, b:b + 1], in1=dst,
                                                       op0=ALU.mult, op1=ALU.add)
                    ins.then_inc(h_out, 1)


def _constants():
    c = np.zeros((P, C_END), np.float32)
    c[:, C_IDENT:C_IDENT + P] = np.eye(P, dtype=np.float32)
    inv_freq = (np.float32(1.0) / np.float32(10000.0) ** (np.arange(P, dtype=np.float32) / np.float32(P)))
    angle = inv_freq.astype(np.float32)[:, None] * np.arange(P, dtype=np.float32)[None, :]
    c[:, C_COS:C_COS + P] = np.cos(angle)
    c[:, C_SIN:C_SIN + P] = np.sin(angle)
    c[:, C_MASK:C_MASK + P] = np.where(np.tril(np.ones((P, P), bool)), 0.0, MASKED)
    c[:, C_HEAD:C_HEAD + H // 2] = (np.arange(P)[:, None] % (H // 2)) == np.arange(H // 2)[None, :]
    c[:, C_SIGN] = np.where(np.arange(P) < 64, -1.0, 1.0)
    return c


def kernel(**inputs):
    import concourse.bacc as bacc
    from concourse.bass_utils import run_bass_kernel_spmd

    a = {k: np.asarray(v) for k, v in inputs.items()}
    ids = np.concatenate([a["x"].T, a["mask_BS_i1_0"].T], axis=1)

    def rows(v):
        return np.broadcast_to(v[None, :], (P, v.shape[0]))

    emb = np.concatenate([a["L0_tok_pos_W"], rows(a["L0_tok_type_W"][0]), rows(a["L0_tok_type_W"][1]),
                          rows(a["L0_tok_ln_w"]), rows(a["L0_tok_ln_b"])], axis=1)
    attn = np.stack([a["L0_attn_w_" + m].reshape(HD, HD, H // 2, 2).transpose(0, 2, 3, 1) for m in "qkv"], axis=2)
    attn = attn.reshape(P, 6, HD)

    f = np.zeros((P, F_END), np.float32)
    w1, w2, gw1 = a["L0_ffn_cn_w1"], a["L0_ffn_cn_w2"], a["L0_ffn_gc_w1"]
    for k in range(2):
        f[:, F_W1 + k * D:F_W1 + (k + 1) * D] = w1[k * P:(k + 1) * P]
        f[:, F_W2 + k * P:F_W2 + (k + 1) * P] = w2[k * P:(k + 1) * P]
        f[:, F_G1 + k * P:F_G1 + (k + 1) * P] = gw1[k * P:(k + 1) * P]
        f[:, F_B1 + k] = a["L0_ffn_cn_b1"][k * P:(k + 1) * P]
    f[:, F_W3:F_W3 + 64] = a["L0_ffn_cn_w3"]
    f[:, F_G2:F_G2 + 64] = a["L0_ffn_gc_w2"]
    f[0:64, F_W4] = a["L0_ffn_cn_w4"][:, 0]
    f[0:64, F_G3] = a["L0_ffn_gc_w3"][:, 0]
    f[:, F_B2] = a["L0_ffn_cn_b2"]
    f[0:64, F_B3] = a["L0_ffn_cn_b3"]
    f[:, F_B4] = a["L0_ffn_cn_b4"][0]
    f[:, F_GB1] = a["L0_ffn_gc_b1"]
    f[0:64, F_GB2] = a["L0_ffn_gc_b2"]
    f[:, F_GB3] = a["L0_ffn_gc_b3"][0]
    f[:, F_AR] = a["L0_ffn_adaptive_range"][0]

    arrays = {"ids": ids, "emb": emb, "consts": _constants(), "attn_w": attn, "ffn_w": f,
              "token_w": a["L0_tok_token_W"]}
    arrays = {k: np.ascontiguousarray(v) for k, v in arrays.items()}
    nc = bacc.Bacc("TRN2", target_bir_lowering=False, num_devices=1)
    args = [nc.dram_tensor(k, v.shape, mybir.dt.from_np(v.dtype), kind="ExternalInput").ap()
            for k, v in arrays.items()]
    out = nc.dram_tensor("out", (NB, P, D), F32, kind="ExternalOutput").ap()
    tower(nc, *args, out)
    r = run_bass_kernel_spmd(nc, [arrays], core_ids=[0])
    return r.results[0]["out"]
```

```python
from contextlib import ExitStack

import numpy as np

import concourse.bass as bass
from concourse import mybir

ALU = mybir.AluOpType
ACT = mybir.ActivationFunctionType
F32 = mybir.dt.float32
I32 = mybir.dt.int32
AX = mybir.AxisListType

P = 128
NB = 16
D = 256
H = 16
HD = D // H
PAIRS = NB // 2
GROUPS = NB // 4
NG = 4 * P
CYCLES = 3
EPS = 1e-5
BASE_COUPLING = 0.1
SCORE_SCALE = 1.0 / 16.0
MASKED = -1e30
FIRST_PAIRS = 4

C_IDENT, C_COS, C_SIN, C_MASK, C_HEAD, C_SIGN = 0, P, 2 * P, 3 * P, 4 * P, 4 * P + H // 2
C_END = C_SIGN + 1
E_POS, E_TYPE0, E_TYPE1, E_LNW, E_LNB = 0, D, 2 * D, 3 * D, 4 * D
F_W1, F_W2, F_W3 = 0, 2 * D, 2 * D + 2 * P
F_G1, F_G2 = F_W3 + 64, F_W3 + 64 + 2 * P
F_W4, F_G3 = F_G2 + 64, F_G2 + 65
F_B1, F_B2, F_B3, F_B4 = F_G3 + 1, F_G3 + 3, F_G3 + 4, F_G3 + 5
F_GB1, F_GB2, F_GB3, F_AR = F_B4 + 1, F_B4 + 2, F_B4 + 3, F_B4 + 4
F_END = F_AR + 1


def tower(nc, ids, emb, consts, attn_w, ffn_w, token_w, out):
    ctx = ExitStack()
    with ctx:
        def sb(name, shape, dt=F32):
            return ctx.enter_context(nc.sbuf_tensor(name, shape, dt))

        def sem(name):
            return ctx.enter_context(nc.semaphore(name))

        ids_sb = sb("ids_sb", [P, 2 * NB], I32)
        emb_sb = sb("emb_sb", [P, 5 * D])
        con = sb("con", [P, C_END])
        aw = sb("aw", [P, 6, HD])
        fw = sb("fw", [P, F_END])
        typef = sb("typef", [P, NB])
        pos0 = sb("pos0", [P, D])
        tdiff = sb("tdiff", [P, D])
        wqkv = sb("wqkv", [P, 6, HD, H // 2])
        w1t = sb("w1t", [P, 2, D])
        w4w = sb("w4w", [64, P])
        g3w = sb("g3w", [64, P])
        half_b4 = sb("half_b4", [P, 1])
        half_gb3 = sb("half_gb3", [P, 1])
        ar03 = sb("ar03", [P, 1])
        ar07 = sb("ar07", [P, 1])
        neg_half = sb("neg_half", [P, 2])
        ones = sb("ones", [64, P])

        h = sb("h", [P, NB, D])
        x2nm = sb("x2nm", [P, NB])
        x2r = sb("x2r", [P, NB])

        st_e = sb("st_e", [P, 2, 6]); mv_e = sb("mv_e", [P, 2, 2]); ve_e = sb("ve_e", [P, 2]); nm_e = sb("nm_e", [P, 2])
        rs_e = sb("rs_e", [P, 2]); nb_e = sb("nb_e", [P, 2])
        st_a = sb("st_a", [P, 2, 6]); mv_a = sb("mv_a", [P, 2, 2]); ve_a = sb("ve_a", [P, 2]); nm_a = sb("nm_a", [P, 2])
        rs_a = sb("rs_a", [P, 2]); nb_a = sb("nb_a", [P, 2])
        st_f = sb("st_f", [P, 2, 6]); mv_f = sb("mv_f", [P, 2, 2]); ve_f = sb("ve_f", [P, 2]); nm_f = sb("nm_f", [P, 2])
        xn = sb("xn", [P, 2, 2, P])
        xT = sb("xT", [P, 2, 2, P])
        tcos = sb("tcos", [P, 2, 2, 2, P])
        tsin = sb("tsin", [P, 2, 2, 2, P])
        rot = sb("rot", [P, 2, 2, 2, P])
        v_sb = sb("v_sb", [P, 2, D])
        sc = sb("sc", [P, 2, P])
        nmax = sb("nmax", [P, 2])
        prob = sb("prob", [P, 2, P])
        psum_row = sb("psum_row", [P, 2])
        rinv = sb("rinv", [P, 2])
        probT = sb("probT", [P, 2, P])
        x2 = sb("x2", [P, 2, D])
        x2T = sb("x2T", [P, 2, 2, P])
        gsum = sb("gsum", [P, 2, NB])

        pre = sb("pre", [P, 2, NB * P])
        tw = sb("tw", [P, 2, NB * P])
        a1 = sb("a1", [P, 2, 2, NG])
        a2 = sb("a2", [P, 2, NG])
        a3 = sb("a3", [64, 2, NG])
        tz = sb("tz", [P, 2, NG])
        cpl = sb("cpl", [P, 2, 4, P])
        up = sb("up", [P, 2, NG])
        ut = sb("ut", [P, 2, 2, NG])
        g1 = sb("g1", [P, NB]); g2 = sb("g2", [64, NB]); tg = sb("tg", [P, NB]); base = sb("base", [P, NB])
        tcol = sb("tcol", [P, CYCLES, NB])
        ccol = sb("ccol", [P, CYCLES, NB])
        cw = sb("cw", [P, 10, NB])
        xf = sb("xf", [P, NB, D])

        banks = [ctx.enter_context(nc.psum_tensor(f"bank{i}", [P, 512], F32)) for i in range(8)]
        tr_ps = banks[0][:, :].rearrange("p (j a t) -> p j a t", j=2, a=2)
        q_ps = banks[1][:, :].rearrange("p (a t) -> p a t", a=2)
        k_ps = banks[2][:, :].rearrange("p (a t) -> p a t", a=2)
        v_ps = banks[3][:, :].rearrange("p (j a i) -> p j a i", j=2, a=2)
        s_ps = banks[4][:, 0:2 * P].rearrange("p (j t) -> p j t", j=2)
        pt_ps = banks[4][:, 2 * P:4 * P].rearrange("p (j t) -> p j t", j=2)
        y_ps = banks[6][:, :].rearrange("p (j d) -> p j d", j=2)
        pre_ps = banks[5][:, :].rearrange("p (m t) -> p m t", m=2)
        tw_ps = banks[7][:, :].rearrange("p (m t) -> p m t", m=2)

        ident = con[:, C_IDENT:C_IDENT + P]
        cos_b = con[:, C_COS:C_COS + P].unsqueeze(1).broadcast_to([P, 4, P])
        sin_b = con[:, C_SIN:C_SIN + P].unsqueeze(1).broadcast_to([P, 4, P])
        mask = con[:, C_MASK:C_MASK + P]
        lnw = emb_sb[:, E_LNW:E_LNW + D]
        lnb = emb_sb[:, E_LNB:E_LNB + D]
        w1 = fw[:, F_W1:F_W1 + 2 * D].rearrange("p (k n) -> p k n", k=2)
        w2 = fw[:, F_W2:F_W2 + 2 * P].rearrange("p (k n) -> p k n", k=2)
        w3 = fw[:, F_W3:F_W3 + 64]
        gw1 = fw[:, F_G1:F_G1 + 2 * P].rearrange("p (k n) -> p k n", k=2)
        gw2 = fw[:, F_G2:F_G2 + 64]

        def w_attn(m, par):
            return wqkv[:, 2 * m + par, :, :].rearrange("p d i -> p (d i)")

        ids_in = sem("ids_in"); emb_in = sem("emb_in"); ln_in = sem("ln_in"); con_in = sem("con_in")
        aw_in = sem("aw_in"); fw_in = sem("fw_in"); out_done = sem("out_done")
        rows_in = [sem(f"rows_in{b}") for b in range(2 * FIRST_PAIRS)]
        rest_in = sem("rest_in")
        prep = sem("prep")
        prefilled = sem("prefilled")
        pool_ready = sem("pool_ready"); wqkv_ready = sem("wqkv_ready"); ffn_ready = sem("ffn_ready"); half_ready = sem("half_ready")
        e_stats = sem("e_stats"); e_mv = sem("e_mv"); e_var = sem("e_var"); e_rstd = sem("e_rstd")
        e_norm = sem("e_norm"); e_scaled = sem("e_scaled"); h0_ready = sem("h0_ready")
        a_stats = sem("a_stats"); a_mv = sem("a_mv"); a_var = sem("a_var"); a_rstd = sem("a_rstd")
        xn_ready = sem("xn_ready")
        xn_turned = sem("xn_turned"); xT_ready = sem("xT_ready")
        q_ready = sem("q_ready"); k_ready = sem("k_ready")
        q_parts = sem("q_parts"); k_parts = sem("k_parts"); rot_ready = sem("rot_ready")
        scored = sem("scored"); sc_ready = sem("sc_ready"); prob_ready = sem("prob_ready")
        prob_turned = sem("prob_turned"); probT_ready = sem("probT_ready")
        v_made = sem("v_made"); v_ready = sem("v_ready"); y_made = sem("y_made")
        rinv_ready = sem("rinv_ready"); h1_ready = sem("h1_ready")
        f_stats = sem("f_stats"); f_mv = sem("f_mv"); f_var = sem("f_var"); f_rstd = sem("f_rstd")
        x2_ready = sem("x2_ready"); x2_turned = sem("x2_turned"); x2T_ready = sem("x2T_ready")
        mean_ready = sem("mean_ready"); x2T_used = sem("x2T_used")
        pre_made = sem("pre_made"); tw_made = sem("tw_made")
        pre_out = sem("pre_out"); tw_out = sem("tw_out")
        g_mm = sem("g_mm"); g_act = sem("g_act"); base_ready = sem("base_ready")
        a1_ready = sem("a1_ready"); l2_made = sem("l2_made"); a2_ready = sem("a2_ready")
        l3_made = sem("l3_made"); a3_ready = sem("a3_ready"); l4_made = sem("l4_made")
        zcol_made = sem("zcol_made")
        tz_ready = sem("tz_ready"); tcol_ready = sem("tcol_ready")
        cpl_ready = sem("cpl_ready"); prod_ready = sem("prod_ready"); pre_new = sem("pre_new")
        tw_new = sem("tw_new"); small = sem("small"); xf_ready = sem("xf_ready")
        mixed = sem("mixed"); h_out = sem("h_out")

        def at_least(eng, s, v):
            if not (isinstance(v, int) and v <= 0):
                eng.wait_ge(s, v)

        def wait_alone(eng, s, v):
            if isinstance(v, int):
                return at_least(eng, s, v)
            v = eng.to_reg(v)
            eng.wait_ge(con_in, 16)
            eng.wait_ge(s, v)

        def phases(eng, body):
            body(-1, "E")
            body(0, "EX")
            body(1, "EXA")
            body(2, "EXAF")
            with eng.Fori(3, PAIRS - 1) as i:
                body(i, "EXAF")
            body(PAIRS - 1, "XAF")
            body(PAIRS, "AF")
            body(PAIRS + 1, "F")

        def twist_update(eng, n):
            eng.wait_ge(prod_ready, 2 * (n + 1))
            cols = slice(n * NG, (n + 1) * NG)
            eng.tensor_tensor(tw[:, :, cols], tw[:, :, cols], ut[:, n % 2, :, :], ALU.subtract).then_inc(tw_new, 1)

        def row_of(b):
            return h[:, bass.ds(b, 1), :].rearrange("p o d -> p (o d)")

        block = ctx.enter_context(nc.Block())

        @block.sync
        def _(sp):
            sp.dma_start(ids_sb[:, :], ids).then_inc(ids_in, 16)
            sp.dma_start(emb_sb[:, 0:E_LNW], emb[:, 0:E_LNW]).then_inc(emb_in, 16)
            sp.dma_start(emb_sb[:, E_LNW:5 * D], emb[:, E_LNW:5 * D]).then_inc(ln_in, 16)
            sp.dma_start(con[:, :], consts).then_inc(con_in, 16)
            sp.dma_start(aw[:, :, :], attn_w).then_inc(aw_in, 16)
            sp.dma_start(fw[:, :], ffn_w).then_inc(fw_in, 16)
            for g in range(GROUPS):
                sp.wait_ge(h_out, 8 * (g + 1))
                sp.dma_start(out[4 * g:4 * g + 4].rearrange("b t d -> t b d"),
                             h[:, 4 * g:4 * g + 4, :]).then_inc(out_done, 16)
            sp.wait_ge(out_done, 16 * GROUPS)

        @block.gpsimd
        def _(pool):
            def gather(b):
                pool.wait_ge(prefilled, b + 1)
                pool.indirect_dma_start(
                    out=h[:, b, :], out_offset=None, in_=token_w,
                    in_offset=bass.IndirectOffsetOnAxis(ap=ids_sb[:, b:b + 1], axis=0),
                    compute_op=ALU.add,
                ).then_inc(rows_in[b] if b < 2 * FIRST_PAIRS else rest_in, 16)

            pool.wait_ge(ids_in, 16)
            pool.wait_ge(ln_in, 16)
            for b in range(4):
                gather(b)
            later = iter(range(4, NB))

            def gather_more(i):
                if isinstance(i, int) and i < 3:
                    for _, b in zip(range(1), later):
                        gather(b)


            def rstd(out_r, out_b, ve, nm, done, ready):
                pool.tensor_tensor(out_r, ve[:, :], neg_half[:, :], ALU.pow).then_inc(ready, 1)
                pool.wait_ge(ready, done + 1)
                pool.tensor_tensor(out_b, nm[:, :], out_r, ALU.mult).then_inc(ready, 1)

            def body(i, what):
                if "E" in what:
                    pool.wait_ge(e_var, 2 * (i + 2))
                    at_least(pool, e_norm, 2 * (i + 1))
                    rstd(rs_e[:, :], nb_e[:, :], ve_e, nm_e, 2 * (i + 1), e_rstd)
                    gather_more(i)
                if "X" in what:
                    pool.wait_ge(q_parts, i + 1)
                    at_least(pool, scored, i)
                    pool.tensor_tensor(rot[:, 0, 0], tcos[:, 0, 0], tsin[:, 0, 1], ALU.subtract).then_inc(rot_ready, 1)
                    pool.tensor_tensor(rot[:, 0, 1], tcos[:, 0, 1], tsin[:, 0, 0], ALU.add).then_inc(rot_ready, 1)
                if "E" in what:
                    for j in range(2):
                        row = h[:, bass.ds(2 * i + 2 + j, 1), :].rearrange("p o d -> p (o d)")
                        pool.wait_ge(e_norm, 2 * (i + 1) + j + 1)
                        pool.tensor_tensor(row, row, lnw, ALU.mult).then_inc(e_scaled, 1)
                    gather_more(i)
                if "X" in what:
                    pool.wait_ge(k_parts, i + 1)
                    pool.tensor_tensor(rot[:, 1, 0], tcos[:, 1, 0], tsin[:, 1, 1], ALU.subtract).then_inc(rot_ready, 1)
                    pool.tensor_tensor(rot[:, 1, 1], tcos[:, 1, 1], tsin[:, 1, 0], ALU.add).then_inc(rot_ready, 1)
                if "E" in what:
                    pool.wait_ge(a_var, 2 * (i + 2))
                    at_least(pool, xn_ready, 2 * (i + 1))
                    rstd(rs_a[:, :], nb_a[:, :], ve_a, nm_a, 2 * (i + 1), a_rstd)
                    gather_more(i)
                    gather_more(i)
                if "A" in what:
                    pool.wait_ge(f_var, 2 * i)
                    cols = bass.ds(2 * i - 2, 2)
                    rstd(x2r[:, cols], x2nm[:, cols], ve_f, nm_f, 2 * (i - 1), f_rstd)
            phases(pool, body)

            pool.wait_ge(base_ready, 1)
            for n in range((CYCLES - 1) * GROUPS):
                g, s = n % GROUPS, n % 2
                pool.wait_ge(tz_ready, n + 1)
                at_least(pool, prod_ready, 2 * (n - 1) if n <= GROUPS else GROUPS + n - 1)
                for j in range(4):
                    ins = pool.tensor_scalar(cpl[:, s, j, :], tz[:, s, j * P:(j + 1) * P], ar03[:, :],
                                             base[:, 4 * g + j:4 * g + j + 1], ALU.mult, ALU.add)
                ins.then_inc(cpl_ready, 1)
                if 1 <= n <= GROUPS:
                    twist_update(pool, n - 1)

        @block.tensor
        def _(pe):
            pe.wait_ge(con_in, 16)

            def body(i, what):
                if "X" in what:
                    pe.wait_ge(xn_ready, 2 * (i + 1))
                    at_least(pe, x2T_ready, i - 2)
                    for j in range(2):
                        for par in range(2):
                            mm = pe.transpose(tr_ps[:, j, par, :], xn[:, j, par, :], ident)
                    mm.then_inc(xn_turned, 1)
                if "A" in what:
                    pe.wait_ge(rot_ready, 4 * i)
                    at_least(pe, probT_ready, i - 1)
                    for j in range(2):
                        for par in range(2):
                            mm = pe.matmul(s_ps[:, j, :], rot[:, 0, par, j, :], rot[:, 1, par, j, :],
                                           start=(par == 0), stop=(par == 1))
                    mm.then_inc(scored, 1)
                if "X" in what:
                    pe.wait_ge(xT_ready, i + 1)
                    if isinstance(i, int) and i == 0:
                        pe.wait_ge(wqkv_ready, 1)
                    for m, (ps, used, made) in enumerate(((q_ps, q_parts, q_ready), (k_ps, k_parts, k_ready))):
                        at_least(pe, used, i)
                        for par in range(2):
                            mm = pe.matmul(ps[:, par, :], w_attn(m, par),
                                           xT[:, par, :, :].rearrange("p j t -> p (j t)"),
                                           start=True, stop=True)
                        mm.then_inc(made, 1)
                if "A" in what:
                    pe.wait_ge(prob_ready, 2 * i)
                    for j in range(2):
                        mm = pe.transpose(pt_ps[:, j, :], prob[:, j, :], ident)
                    mm.then_inc(prob_turned, 1)
                if "X" in what:
                    at_least(pe, v_ready, i)
                    for j in range(2):
                        for par in range(2):
                            mm = pe.matmul(v_ps[:, j, par, :], xT[:, par, j, :], w_attn(2, par),
                                           start=True, stop=True)
                    mm.then_inc(v_made, 1)
                if "F" in what:
                    pe.wait_ge(x2_ready, 2 * (i - 1))
                    if "X" in what:
                        pe.wait_ge(xT_ready, i + 1)
                    else:
                        at_least(pe, x2T_ready, i - 2)
                    for j in range(2):
                        for a in range(2):
                            mm = pe.transpose(tr_ps[:, j, a, :], x2[:, j, a * P:(a + 1) * P], ident)
                    mm.then_inc(x2_turned, 1)
                if "A" in what:
                    pe.wait_ge(probT_ready, i)
                    pe.wait_ge(v_ready, i)
                    at_least(pe, h1_ready, 2 * (i - 1))
                    for j in range(2):
                        mm = pe.matmul(y_ps[:, j, :], probT[:, j, :], v_sb[:, j, :], start=True, stop=True)
                    mm.then_inc(y_made, 1)
                if "F" in what:
                    pe.wait_ge(x2T_ready, i - 1)
                    if isinstance(i, int) and i == 2 or not isinstance(i, int):
                        pe.wait_ge(ffn_ready, 4)
                    for w, ps, left, made in ((w1, pre_ps, pre_out, pre_made), (w1t, tw_ps, tw_out, tw_made)):
                        at_least(pe, left, i - 2)
                        for m in range(2):
                            for k in range(2):
                                mm = pe.matmul(ps[:, m, :], w[:, k, m * P:(m + 1) * P],
                                               x2T[:, k, :, :].rearrange("p j t -> p (j t)"),
                                               start=(k == 0), stop=(k == 1))
                        mm.then_inc(made, 1)

            phases(pe, body)

            items = CYCLES * GROUPS
            for n in range(items + 2):
                if n >= 2:
                    m = n - 2
                    pe.wait_ge(a3_ready, m + 1)
                    if m == 1:
                        pe.wait_ge(g_act, 3)
                    if m < items - GROUPS:
                        at_least(pe, tz_ready, m - 1)
                        pe.matmul(banks[4 + m % 2][:, :], w4w[:, :], a3[:, m % 2, :],
                                  start=True, stop=True).then_inc(l4_made, 1)
                    at_least(pe, tcol_ready, m - 1)
                    for j in range(4):
                        mm = pe.matmul(banks[6 + m % 2][:, j:j + 1], a3[:, m % 2, j * P:(j + 1) * P],
                                       fw[0:64, F_W4:F_W4 + 1], start=True, stop=True)
                    mm.then_inc(zcol_made, 1)
                if 1 <= n <= items:
                    pe.wait_ge(a2_ready, n)
                    at_least(pe, a3_ready, n - 2)
                    pe.matmul(banks[2 + (n - 1) % 2][0:64, :], w3, a2[:, (n - 1) % 2, :],
                              start=True, stop=True).then_inc(l3_made, 1)
                if n < items:
                    pe.wait_ge(a1_ready, n + 1)
                    at_least(pe, a2_ready, n - 1)
                    for k in range(2):
                        mm = pe.matmul(banks[n % 2][:, :], w2[:, k, :], a1[:, n % 2, k, :],
                                       start=(k == 0), stop=(k == 1))
                    mm.then_inc(l2_made, 1)
                if n == 0:
                    pe.wait_ge(mean_ready, PAIRS)
                    for k in range(2):
                        mm = pe.matmul(banks[6][:, 0:NB], gw1[:, k, :], gsum[:, k, :], start=(k == 0), stop=(k == 1))
                    mm.then_inc(g_mm, 1)
                if n == 1:
                    pe.wait_ge(g_act, 1)
                    pe.wait_ge(tw_out, PAIRS)
                    pe.matmul(banks[7][0:64, 0:NB], gw2, g1[:, :], start=True, stop=True).then_inc(g_mm, 1)
                if n == 2:
                    pe.wait_ge(g_act, 2)
                    pe.wait_ge(pre_out, PAIRS)
                    pe.matmul(banks[5][:, 0:NB], g3w[:, :], g2[:, :], start=True, stop=True).then_inc(g_mm, 1)

        @block.scalar
        def _(act):
            items = CYCLES * GROUPS

            def first(n):
                g = n % GROUPS
                if n < GROUPS:
                    act.wait_ge(pre_out, 2 * (g + 1))
                else:
                    act.wait_ge(pre_new, n - GROUPS + 1)
                at_least(act, l2_made, n - 1)
                for k in range(2):
                    ins = act.activation(a1[:, n % 2, k, :], pre[:, k, g * NG:(g + 1) * NG], ACT.Gelu,
                                         bias=fw[:, F_B1 + k:F_B1 + k + 1])
                ins.then_inc(a1_ready, 1)

            def body(i, what):
                if "X" in what:
                    act.wait_ge(xn_turned, i + 1)
                    at_least(act, v_made, i)
                    act.activation(xT[:, :, :, :], tr_ps.rearrange("p j a t -> p a j t"),
                                   ACT.Copy).then_inc(xT_ready, 1)
                if "A" in what:
                    for j in range(2):
                        act.wait_ge(sc_ready, 2 * (i - 1) + j + 1)
                        if j == 0:
                            at_least(act, prob_turned, i - 1)
                            at_least(act, rinv_ready, i - 1)
                        act.activation(prob[:, j, :], sc[:, j, :], ACT.Exp, bias=nmax[:, j:j + 1], scale=-1.0,
                                       accum_out=psum_row[:, j:j + 1]).then_inc(prob_ready, 1)
                if "F" in what:
                    wait_alone(act, f_rstd, 2 * (i - 1))
                    wait_alone(act, x2_turned, i - 2)
                    for j in range(2):
                        act.activation(x2[:, j, :], row_of(2 * i - 4 + j), ACT.Identity,
                                       bias=x2nm[:, bass.ds(2 * i - 4 + j, 1)],
                                       scale=x2r[:, bass.ds(2 * i - 4 + j, 1)]).then_inc(x2_ready, 1)
                if "A" in what:
                    act.wait_ge(prob_turned, i)
                    at_least(act, y_made, i - 1)
                    act.activation(probT[:, :, :], pt_ps, ACT.Copy).then_inc(probT_ready, 1)
                if "E" in what:
                    wait_alone(act, e_rstd, 2 * (i + 2))
                    for j in range(2):
                        act.activation(row_of(2 * i + 2 + j), row_of(2 * i + 2 + j), ACT.Identity,
                                       bias=nb_e[:, j:j + 1], scale=rs_e[:, j:j + 1]).then_inc(e_norm, 1)
                if "F" in what:
                    act.wait_ge(x2_turned, i - 1)
                    at_least(act, tw_made, i - 2)
                    at_least(act, mean_ready, i - 2)
                    act.activation(x2T[:, :, :, :], tr_ps.rearrange("p j a t -> p a j t"),
                                   ACT.Copy).then_inc(x2T_ready, 1)
                if "X" in what:
                    act.wait_ge(v_made, i + 1)
                    at_least(act, y_made, i)
                    act.activation(v_sb[:, :, :].rearrange("p j (i a) -> p j a i", a=2), v_ps,
                                   ACT.Copy).then_inc(v_ready, 1)
                if "E" in what:
                    wait_alone(act, a_rstd, 2 * (i + 2))
                    wait_alone(act, xn_turned, i + 1)
                    for j in range(2):
                        act.activation(xn[:, j, :, :], row_of(2 * i + 2 + j).rearrange("p (i a) -> p a i", a=2),
                                       ACT.Identity, bias=nb_a[:, j:j + 1],
                                       scale=rs_a[:, j:j + 1]).then_inc(xn_ready, 1)
                if "X" not in what and "A" not in what and "F" in what:
                    act.wait_ge(fw_in, 16)
                    first(0)
                if "F" in what:
                    act.wait_ge(pre_made, i - 1)
                    act.activation(pre[:, :, bass.ds((i - 2) * (2 * P), 2 * P)], pre_ps, ACT.Copy).then_inc(pre_out, 1)
                    act.wait_ge(tw_made, i - 1)
                    act.activation(tw[:, :, bass.ds((i - 2) * (2 * P), 2 * P)], tw_ps, ACT.Copy).then_inc(tw_out, 1)

            phases(act, body)

            act.wait_ge(half_ready, 2)

            def last(m):
                g = m % GROUPS
                if m < items - GROUPS:
                    act.wait_ge(l4_made, m + 1)
                    at_least(act, cpl_ready, m - 1)
                    act.activation(tz[:, m % 2, :], banks[4 + m % 2][:, :], ACT.Tanh, bias=half_b4[:, :],
                                   scale=0.5).then_inc(tz_ready, 1)
                act.wait_ge(zcol_made, m + 1)
                act.activation(tcol[:, m // GROUPS, 4 * g:4 * g + 4], banks[6 + m % 2][:, 0:4], ACT.Tanh,
                               bias=half_b4[:, :], scale=0.5).then_inc(tcol_ready, 1)

            for n in range(items + 2):
                if n >= 2:
                    last(n - 2)
                if n + 1 < items:
                    first(n + 1)
                if 1 <= n <= items:
                    act.wait_ge(l3_made, n)
                    at_least(act, zcol_made, n - 2)
                    act.activation(a3[:, (n - 1) % 2, :], banks[2 + (n - 1) % 2][0:64, :], ACT.Gelu,
                                   bias=fw[0:64, F_B3:F_B3 + 1]).then_inc(a3_ready, 1)
                if n < items:
                    act.wait_ge(l2_made, n + 1)
                    at_least(act, l3_made, n - 1)
                    act.activation(a2[:, n % 2, :], banks[n % 2][:, :], ACT.Gelu,
                                   bias=fw[:, F_B2:F_B2 + 1]).then_inc(a2_ready, 1)
                if n == 0:
                    act.wait_ge(g_mm, 1)
                    act.activation(g1[:, :], banks[6][:, 0:NB], ACT.Gelu, bias=fw[:, F_GB1:F_GB1 + 1],
                                   scale=1.0 / P).then_inc(g_act, 1)
                if n == 1:
                    act.wait_ge(g_mm, 2)
                    act.activation(g2[:, :], banks[7][0:64, 0:NB], ACT.Gelu,
                                   bias=fw[0:64, F_GB2:F_GB2 + 1]).then_inc(g_act, 1)
                if n == 2:
                    act.wait_ge(g_mm, 3)
                    act.activation(tg[:, :], banks[5][:, 0:NB], ACT.Tanh, bias=half_gb3[:, :],
                                   scale=0.5).then_inc(g_act, 1)
                if items - GROUPS - 2 <= n < items - 2:
                    g = n - (items - GROUPS - 2)
                    for b in range(4 * g, 4 * g + 4):
                        ins = act.activation(xf[:, b, :], h[:, b, :], ACT.Identity, bias=x2nm[:, b:b + 1],
                                             scale=x2r[:, b:b + 1])
                    ins.then_inc(xf_ready, 1)

        @block.vector
        def _(dve):
            dve.memset(neg_half[:, :], -0.5).then_inc(prep, 1)
            dve.memset(ones[:, :], 1.0).then_inc(prep, 1)
            dve.wait_ge(ids_in, 16)
            dve.tensor_copy(typef[:, :], ids_sb[:, NB:2 * NB]).then_inc(prep, 1)
            dve.wait_ge(emb_in, 16)
            dve.tensor_tensor(pos0[:, :], emb_sb[:, E_POS:E_POS + D], emb_sb[:, E_TYPE0:E_TYPE0 + D],
                              ALU.add).then_inc(prep, 1)
            dve.tensor_tensor(tdiff[:, :], emb_sb[:, E_TYPE1:E_TYPE1 + D], emb_sb[:, E_TYPE0:E_TYPE0 + D],
                              ALU.subtract).then_inc(prep, 1)
            dve.wait_ge(prep, 5)
            def prefill(rows):
                for b in rows:
                    dve.scalar_tensor_tensor(out=h[:, b, :], in0=tdiff[:, :], scalar=typef[:, b:b + 1],
                                             in1=pos0[:, :], op0=ALU.mult, op1=ALU.add).then_inc(prefilled, 1)

            prefill(range(4))
            dve.wait_ge(ln_in, 16)
            dve.wait_ge(con_in, 16)
            dve.wait_ge(aw_in, 16)
            head = con[:, C_HEAD:C_HEAD + H // 2]
            dve.tensor_tensor(wqkv[:, :, :, :].rearrange("p m d i -> p (m d) i"),
                              aw[:, :, :].rearrange("p m d -> p (m d)").unsqueeze(2).broadcast_to([P, 6 * HD, H // 2]),
                              head.unsqueeze(1).broadcast_to([P, 6 * HD, H // 2]),
                              ALU.mult).then_inc(wqkv_ready, 1)
            dve.wait_ge(fw_in, 16)
            sign = con[:, C_SIGN:C_SIGN + 1]
            dve.tensor_scalar(w1t[:, 0, :], w1[:, 1, :], sign, None, ALU.mult).then_inc(ffn_ready, 1)
            dve.tensor_scalar(w1t[:, 1, :], w1[:, 0, :], sign, -1.0, ALU.mult, ALU.mult).then_inc(ffn_ready, 1)
            dve.tensor_scalar(w4w[:, :], ones[:, :], fw[0:64, F_W4:F_W4 + 1], None, ALU.mult).then_inc(ffn_ready, 1)
            dve.tensor_scalar(g3w[:, :], ones[:, :], fw[0:64, F_G3:F_G3 + 1], None, ALU.mult).then_inc(ffn_ready, 1)
            dve.tensor_scalar(half_b4[:, :], fw[:, F_B4:F_B4 + 1], 0.5, None, ALU.mult).then_inc(half_ready, 1)
            dve.tensor_scalar(half_gb3[:, :], fw[:, F_GB3:F_GB3 + 1], 0.5, None, ALU.mult).then_inc(half_ready, 1)
            dve.tensor_scalar(ar03[:, :], fw[:, F_AR:F_AR + 1], 0.3, None, ALU.mult).then_inc(prep, 1)
            dve.tensor_scalar(ar07[:, :], fw[:, F_AR:F_AR + 1], 0.7, None, ALU.mult).then_inc(prep, 1)

            def layernorm_stats(rows, st, mv, ve, nm, stats, mvs, var, done):
                for j in range(2):
                    dve.bn_stats(st[:, j, :], rows[j]).then_inc(stats, 1)
                for j in range(2):
                    wait_alone(dve, stats, 2 * done + j + 1)
                    dve.bn_aggr(mv[:, j, :], st[:, j, :]).then_inc(mvs, 1)
                dve.wait_ge(mvs, 2 * done + 2)
                dve.tensor_scalar(ve[:, :], mv[:, :, 1], EPS, None, ALU.add).then_inc(var, 1)
                dve.tensor_scalar(nm[:, :], mv[:, :, 0], -1.0, None, ALU.mult).then_inc(var, 1)

            def body(i, what):
                if "E" in what:
                    if isinstance(i, int):
                        if i < FIRST_PAIRS - 1:
                            for j in range(2):
                                dve.wait_ge(rows_in[2 * (i + 1) + j], 16)
                    rows = [row_of(2 * i + 2), row_of(2 * i + 3)]
                    layernorm_stats(rows, st_e, mv_e, ve_e, nm_e, e_stats, e_mv, e_var, i + 1)
                    if isinstance(i, int) and i == -1:
                        prefill(range(4, NB))
                if "A" in what:
                    wait_alone(dve, prob_ready, 2 * (i - 1))
                    wait_alone(dve, scored, i)
                    for j in range(2):
                        dve.tensor_tensor_reduce(sc[:, j, :], s_ps[:, j, :], mask, -SCORE_SCALE, 3e38,
                                                 ALU.add, ALU.min, nmax[:, j:j + 1]).then_inc(sc_ready, 1)
                if "X" in what:
                    for m, (made, parts) in enumerate(((q_ready, q_parts), (k_ready, k_parts))):
                        dve.wait_ge(made, i + 1)
                        if m == 0:
                            at_least(dve, rot_ready, 4 * i)
                        ps = banks[1 + m][:, :].rearrange("p (c t) -> p c t", c=4)
                        dve.tensor_tensor(tcos[:, m].rearrange("p a j t -> p (a j) t"), ps, cos_b, ALU.mult)
                        dve.tensor_tensor(tsin[:, m].rearrange("p a j t -> p (a j) t"), ps, sin_b,
                                          ALU.mult).then_inc(parts, 1)
                if "E" in what:
                    for j in range(2):
                        dve.wait_ge(e_scaled, 2 * (i + 1) + j + 1)
                        dve.tensor_tensor(rows[j], rows[j], lnb, ALU.add).then_inc(h0_ready, 1)
                    wait_alone(dve, h0_ready, 2 * (i + 2))
                    layernorm_stats(rows, st_a, mv_a, ve_a, nm_a, a_stats, a_mv, a_var, i + 1)
                if "A" in what:
                    dve.wait_ge(prob_ready, 2 * i)
                    dve.reciprocal(rinv[:, :], psum_row[:, :]).then_inc(rinv_ready, 1)
                    dve.wait_ge(rinv_ready, i)
                    dve.wait_ge(y_made, i)
                    mine = [row_of(2 * i - 2), row_of(2 * i - 1)]
                    for j in range(2):
                        dve.scalar_tensor_tensor(out=mine[j], in0=y_ps[:, j, :], scalar=rinv[:, j:j + 1],
                                                 in1=mine[j], op0=ALU.mult, op1=ALU.add).then_inc(h1_ready, 1)
                    wait_alone(dve, h1_ready, 2 * i)
                    layernorm_stats(mine, st_f, mv_f, ve_f, nm_f, f_stats, f_mv, f_var, i - 1)
                if "F" in what:
                    dve.wait_ge(x2T_ready, i - 1)
                    dve.tensor_reduce(gsum[:, :, bass.ds(2 * i - 4, 2)], x2T[:, :, :, :], AX.X,
                                      ALU.add).then_inc(mean_ready, 1)
                if isinstance(i, int) and i == FIRST_PAIRS - 2:
                    dve.wait_ge(rest_in, 16 * (NB - 2 * FIRST_PAIRS))

            phases(dve, body)

            dve.wait_ge(g_act, 3)
            dve.wait_ge(prep, 7)
            dve.tensor_scalar(base[:, :], tg[:, :], ar07[:, :], BASE_COUPLING, ALU.mult,
                              ALU.add).then_inc(base_ready, 1)
            dve.wait_ge(base_ready, 1)
            updates = (CYCLES - 1) * GROUPS

            def update(n):
                g, s = n % GROUPS, n % 2
                cols = slice(g * NG, (g + 1) * NG)
                full = n < GROUPS
                dve.wait_ge(cpl_ready, n + 1)
                c = cpl[:, s].rearrange("p j t -> p (j t)").unsqueeze(1).broadcast_to([P, 2, NG])
                at_least(dve, pre_new, n)
                if full:
                    dve.wait_ge(tw_out, 2 * (g + 1))
                    at_least(dve, tw_new, n - 1)
                else:
                    dve.wait_ge(tw_new, g + 1)
                dve.tensor_tensor(up[:, :, :], tw[:, :, cols], c, ALU.mult).then_inc(prod_ready, 1)
                if full:
                    dve.tensor_tensor(ut[:, n % 2, :, :], pre[:, :, cols], c, ALU.mult).then_inc(prod_ready, 1)
                dve.wait_ge(prod_ready, 2 * (n + 1) if full else GROUPS + n + 1)
                dve.wait_ge(a1_ready, n + 1)
                dve.tensor_tensor(pre[:, :, cols], pre[:, :, cols], up[:, :, :], ALU.add).then_inc(pre_new, 1)

            steps = [0]

            def step(ins, wait=True):
                ins.then_inc(small, 1)
                steps[0] += 1
                if wait:
                    dve.wait_ge(small, steps[0])

            for n in range(updates):
                update(n)
            dve.wait_ge(tcol_ready, updates)
            c12, alpha2, beta2, c3b, c3a, alpha, beta, nbeta, scale, bias = (cw[:, k, :] for k in range(10))
            c1, c2, c3 = (ccol[:, k, :] for k in range(CYCLES))
            step(dve.scalar_tensor_tensor(out=ccol[:, 0:2, :], in0=tcol[:, 0:2, :], scalar=ar03[:, :],
                                          in1=base[:, :].unsqueeze(1).broadcast_to([P, 2, NB]),
                                          op0=ALU.mult, op1=ALU.add))
            step(dve.tensor_tensor(c12, c1, c2, ALU.mult))
            step(dve.tensor_scalar(alpha2, c12, -1.0, 1.0, ALU.mult, ALU.add), wait=False)
            step(dve.tensor_tensor(beta2, c1, c2, ALU.add))
            for g in range(GROUPS):
                q = slice(4 * g, 4 * g + 4)
                dve.wait_ge(tcol_ready, updates + g + 1)
                step(dve.scalar_tensor_tensor(out=c3[:, q], in0=tcol[:, 2, q], scalar=ar03[:, :],
                                              in1=base[:, q], op0=ALU.mult, op1=ALU.add))
                step(dve.tensor_tensor(c3b[:, q], c3[:, q], beta2[:, q], ALU.mult), wait=False)
                step(dve.tensor_tensor(c3a[:, q], c3[:, q], alpha2[:, q], ALU.mult))
                step(dve.tensor_tensor(alpha[:, q], alpha2[:, q], c3b[:, q], ALU.subtract), wait=False)
                step(dve.tensor_tensor(beta[:, q], beta2[:, q], c3a[:, q], ALU.add))
                step(dve.tensor_scalar(nbeta[:, q], beta[:, q], -1.0, None, ALU.mult))
                dve.wait_ge(xf_ready, g + 1)
                for b in range(4 * g, 4 * g + 4):
                    dve.scalar_tensor_tensor(out=h[:, b, :], in0=xf[:, b, :], scalar=alpha[:, b:b + 1],
                                             in1=h[:, b, :], op0=ALU.mult, op1=ALU.add).then_inc(mixed, 1)
                for b in range(4 * g, 4 * g + 4):
                    dve.wait_ge(mixed, b + 1)
                    hq = h[:, b, :].rearrange("p (q f) -> p q f", q=4)
                    xq = xf[:, b, :].rearrange("p (q f) -> p q f", q=4)
                    dve.scalar_tensor_tensor(out=hq[:, 0::3, :], in0=xq[:, 2:0:-1, :], scalar=beta[:, b:b + 1],
                                             in1=hq[:, 0::3, :], op0=ALU.mult, op1=ALU.add).then_inc(h_out, 1)
                    dve.scalar_tensor_tensor(out=hq[:, 1:3, :], in0=xq[:, 3::-3, :], scalar=nbeta[:, b:b + 1],
                                             in1=hq[:, 1:3, :], op0=ALU.mult, op1=ALU.add).then_inc(h_out, 1)


def _constants():
    c = np.zeros((P, C_END), np.float32)
    c[:, C_IDENT:C_IDENT + P] = np.eye(P, dtype=np.float32)
    inv_freq = (np.float32(1.0) / np.float32(10000.0) ** (np.arange(P, dtype=np.float32) / np.float32(P)))
    angle = inv_freq.astype(np.float32)[:, None] * np.arange(P, dtype=np.float32)[None, :]
    c[:, C_COS:C_COS + P] = np.cos(angle)
    c[:, C_SIN:C_SIN + P] = np.sin(angle)
    c[:, C_MASK:C_MASK + P] = np.where(np.tril(np.ones((P, P), bool)), 0.0, MASKED)
    c[:, C_HEAD:C_HEAD + H // 2] = (np.arange(P)[:, None] % (H // 2)) == np.arange(H // 2)[None, :]
    c[:, C_SIGN] = np.where(np.arange(P) < 64, -1.0, 1.0)
    return c


def kernel(**inputs):
    import concourse.bacc as bacc
    from concourse.bass_utils import run_bass_kernel_spmd

    a = {k: np.asarray(v) for k, v in inputs.items()}
    ids = np.concatenate([a["x"].T, a["mask_BS_i1_0"].T], axis=1)

    def rows(v):
        return np.broadcast_to(v[None, :], (P, v.shape[0]))

    emb = np.concatenate([a["L0_tok_pos_W"], rows(a["L0_tok_type_W"][0]), rows(a["L0_tok_type_W"][1]),
                          rows(a["L0_tok_ln_w"]), rows(a["L0_tok_ln_b"])], axis=1)
    attn = np.stack([a["L0_attn_w_" + m].reshape(HD, HD, H // 2, 2).transpose(0, 2, 3, 1) for m in "qkv"], axis=2)
    attn = attn.reshape(P, 6, HD)

    f = np.zeros((P, F_END), np.float32)
    w1, w2, gw1 = a["L0_ffn_cn_w1"], a["L0_ffn_cn_w2"], a["L0_ffn_gc_w1"]
    for k in range(2):
        f[:, F_W1 + k * D:F_W1 + (k + 1) * D] = w1[k * P:(k + 1) * P]
        f[:, F_W2 + k * P:F_W2 + (k + 1) * P] = w2[k * P:(k + 1) * P]
        f[:, F_G1 + k * P:F_G1 + (k + 1) * P] = gw1[k * P:(k + 1) * P]
        f[:, F_B1 + k] = a["L0_ffn_cn_b1"][k * P:(k + 1) * P]
    f[:, F_W3:F_W3 + 64] = a["L0_ffn_cn_w3"]
    f[:, F_G2:F_G2 + 64] = a["L0_ffn_gc_w2"]
    f[0:64, F_W4] = a["L0_ffn_cn_w4"][:, 0]
    f[0:64, F_G3] = a["L0_ffn_gc_w3"][:, 0]
    f[:, F_B2] = a["L0_ffn_cn_b2"]
    f[0:64, F_B3] = a["L0_ffn_cn_b3"]
    f[:, F_B4] = a["L0_ffn_cn_b4"][0]
    f[:, F_GB1] = a["L0_ffn_gc_b1"]
    f[0:64, F_GB2] = a["L0_ffn_gc_b2"]
    f[:, F_GB3] = a["L0_ffn_gc_b3"][0]
    f[:, F_AR] = a["L0_ffn_adaptive_range"][0]

    arrays = {"ids": ids, "emb": emb, "consts": _constants(), "attn_w": attn, "ffn_w": f,
              "token_w": a["L0_tok_token_W"]}
    arrays = {k: np.ascontiguousarray(v) for k, v in arrays.items()}
    nc = bacc.Bacc("TRN2", target_bir_lowering=False, num_devices=1)
    args = [nc.dram_tensor(k, v.shape, mybir.dt.from_np(v.dtype), kind="ExternalInput").ap()
            for k, v in arrays.items()]
    out = nc.dram_tensor("out", (NB, P, D), F32, kind="ExternalOutput").ap()
    tower(nc, *args, out)
    r = run_bass_kernel_spmd(nc, [arrays], core_ids=[0])
    return r.results[0]["out"]
```

```python
from contextlib import ExitStack

import numpy as np

import concourse.bass as bass
from concourse import mybir

ALU = mybir.AluOpType
ACT = mybir.ActivationFunctionType
F32 = mybir.dt.float32
I32 = mybir.dt.int32
AX = mybir.AxisListType

P = 128
NB = 16
D = 256
H = 16
HD = D // H
PAIRS = NB // 2
GROUPS = NB // 4
NG = 4 * P
CYCLES = 3
EPS = 1e-5
BASE_COUPLING = 0.1
SCORE_SCALE = 1.0 / 16.0
MASKED = -1e30
FIRST_ROWS = 6
FIRST_PAIRS = 5

C_IDENT, C_COS, C_SIN, C_MASK, C_HEAD, C_SIGN = 0, P, 2 * P, 3 * P, 4 * P, 4 * P + H // 2
C_END = C_SIGN + 2
E_POS, E_TYPE0, E_TYPE1, E_LNW, E_LNB = 0, D, 2 * D, 3 * D, 4 * D
F_W1, F_W2, F_W3 = 0, 2 * D, 2 * D + 2 * P
F_G1, F_G2 = F_W3 + 64, F_W3 + 64 + 2 * P
F_W4, F_G3 = F_G2 + 64, F_G2 + 65
F_B1, F_B2, F_B3, F_B4 = F_G3 + 1, F_G3 + 3, F_G3 + 4, F_G3 + 5
F_GB1, F_GB2, F_GB3, F_AR = F_B4 + 1, F_B4 + 2, F_B4 + 3, F_B4 + 4
F_END = F_AR + 1
F_SCALE, F_BIAS, F_BETA, F_NBETA = range(4)


def tower(nc, ids, emb, consts, attn_w, ffn_w, token_w, out):
    ctx = ExitStack()
    with ctx:
        def sb(name, shape, dt=F32):
            return ctx.enter_context(nc.sbuf_tensor(name, shape, dt))

        def sem(name):
            return ctx.enter_context(nc.semaphore(name))

        ids_sb = sb("ids_sb", [P, 2 * NB], I32)
        emb_sb = sb("emb_sb", [P, 5 * D])
        con = sb("con", [P, C_END])
        aw = sb("aw", [P, 6, HD])
        fw = sb("fw", [P, F_END])
        typef = sb("typef", [P, NB])
        pos0 = sb("pos0", [P, D])
        place = sb("place", [P, FIRST_ROWS, D])
        tdiff = sb("tdiff", [P, D])
        wqkv = sb("wqkv", [P, 6, HD, H // 2])
        w1t = sb("w1t", [P, 2, D])
        w4w = sb("w4w", [64, P])
        g3w = sb("g3w", [64, P])
        half_b4 = sb("half_b4", [P, 1])
        half_gb3 = sb("half_gb3", [P, 1])
        ar03 = sb("ar03", [P, 1])
        ar07 = sb("ar07", [P, 1])
        neg_half = sb("neg_half", [P, 2])
        ones = sb("ones", [64, P])

        h = sb("h", [P, NB, D])
        x2nm = sb("x2nm", [P, NB])
        x2r = sb("x2r", [P, NB])

        st_e = sb("st_e", [P, 2, 6]); mv_e = sb("mv_e", [P, 2, 2]); ve_e = sb("ve_e", [P, 2]); nm_e = sb("nm_e", [P, 2])
        rs_e = sb("rs_e", [P, 2]); nb_e = sb("nb_e", [P, 2])
        st_a = sb("st_a", [P, 2, 6]); mv_a = sb("mv_a", [P, 2, 2]); ve_a = sb("ve_a", [P, 2]); nm_a = sb("nm_a", [P, 2])
        rs_a = sb("rs_a", [P, 2]); nb_a = sb("nb_a", [P, 2])
        st_f = sb("st_f", [P, 2, 6]); mv_f = sb("mv_f", [P, 2, 2]); ve_f = sb("ve_f", [P, 2]); nm_f = sb("nm_f", [P, 2])
        xn = sb("xn", [P, 2, 2, P])
        xT = sb("xT", [P, 2, 2, P])
        tcos = sb("tcos", [P, 2, 2, 2, P])
        tsin = sb("tsin", [P, 2, 2, 2, P])
        rot = sb("rot", [P, 2, 2, 2, P])
        v_sb = sb("v_sb", [P, 2, D])
        sc = sb("sc", [P, 2, P])
        nmax = sb("nmax", [P, 2])
        prob = sb("prob", [P, 2, P])
        psum_row = sb("psum_row", [P, 2])
        rinv = sb("rinv", [P, 2])
        probT = sb("probT", [P, 2, P])
        x2 = sb("x2", [P, 2, D])
        x2T = sb("x2T", [P, 2, 2, P])
        gsum = sb("gsum", [P, 2, NB])

        pre = sb("pre", [P, 2, NB * P])
        tw = sb("tw", [P, 2, NB * P])
        a1 = sb("a1", [P, 2, 2, NG])
        a2 = sb("a2", [P, 2, NG])
        a3 = sb("a3", [64, 2, NG])
        tz = sb("tz", [P, 2, NG])
        cpl = sb("cpl", [P, 2, 4, P])
        up = sb("up", [P, 2, 2, NG])
        ut = sb("ut", [P, 2, NG])
        g1 = sb("g1", [P, NB]); g2 = sb("g2", [64, NB]); tg = sb("tg", [P, NB]); base = sb("base", [P, NB])
        tcol = sb("tcol", [P, CYCLES, NB])
        ccol = sb("ccol", [P, CYCLES, NB])
        c12 = sb("c12", [P, NB])
        fix = sb("fix", [P, 4, NB])
        slope = sb("slope", [P, 4, NB])
        part = sb("part", [P, 4, 4])
        fac = sb("fac", [P, 2, 4, 4])
        xf = sb("xf", [P, NB, D])

        banks = [ctx.enter_context(nc.psum_tensor(f"bank{i}", [P, 512], F32)) for i in range(8)]
        tr_ps = banks[0][:, :].rearrange("p (j a t) -> p j a t", j=2, a=2)
        q_ps = banks[1][:, :].rearrange("p (a t) -> p a t", a=2)
        k_ps = banks[2][:, :].rearrange("p (a t) -> p a t", a=2)
        v_ps = banks[3][:, :].rearrange("p (j a i) -> p j a i", j=2, a=2)
        s_ps = banks[4][:, 0:2 * P].rearrange("p (j t) -> p j t", j=2)
        pt_ps = banks[4][:, 2 * P:4 * P].rearrange("p (j t) -> p j t", j=2)
        y_ps = banks[6][:, :].rearrange("p (j d) -> p j d", j=2)
        pre_ps = banks[5][:, :].rearrange("p (m t) -> p m t", m=2)
        tw_ps = banks[7][:, :].rearrange("p (m t) -> p m t", m=2)

        l2_ps = (banks[1], banks[2])
        l3_ps = (banks[3], banks[4])
        l4_ps = (banks[0], banks[5])
        zcol_ps = (banks[7], banks[6])
        g_ps = banks[6]

        ident = con[:, C_IDENT:C_IDENT + P]
        cos_b = con[:, C_COS:C_COS + P].unsqueeze(1).broadcast_to([P, 4, P])
        sin_b = con[:, C_SIN:C_SIN + P].unsqueeze(1).broadcast_to([P, 4, P])
        mask = con[:, C_MASK:C_MASK + P]
        lnw = emb_sb[:, E_LNW:E_LNW + D]
        lnb = emb_sb[:, E_LNB:E_LNB + D]
        w1 = fw[:, F_W1:F_W1 + 2 * D].rearrange("p (k n) -> p k n", k=2)
        w2 = fw[:, F_W2:F_W2 + 2 * P].rearrange("p (k n) -> p k n", k=2)
        w3 = fw[:, F_W3:F_W3 + 64]
        gw1 = fw[:, F_G1:F_G1 + 2 * P].rearrange("p (k n) -> p k n", k=2)
        gw2 = fw[:, F_G2:F_G2 + 64]

        def w_attn(m, par):
            return wqkv[:, 2 * m + par, :, :].rearrange("p d i -> p (d i)")

        ids_in = sem("ids_in"); emb_in = sem("emb_in"); ln_in = sem("ln_in"); con_in = sem("con_in")
        aw_in = sem("aw_in"); fw_in = sem("fw_in"); out_done = sem("out_done")
        rows_in = [sem(f"rows_in{b}") for b in range(2 * FIRST_PAIRS)]
        rest_in = sem("rest_in")
        prep = sem("prep")
        place_ready = sem("place_ready"); placed = sem("placed")
        prefilled = sem("prefilled")
        wqkv_ready = sem("wqkv_ready"); ffn_ready = sem("ffn_ready"); scalars_ready = sem("scalars_ready")
        e_stats = sem("e_stats"); e_mv = sem("e_mv"); e_var = sem("e_var"); e_rstd = sem("e_rstd")
        e_norm = sem("e_norm"); e_scaled = sem("e_scaled"); h0_ready = sem("h0_ready")
        a_stats = sem("a_stats"); a_mv = sem("a_mv"); a_var = sem("a_var"); a_rstd = sem("a_rstd")
        xn_ready = sem("xn_ready")
        xn_turned = sem("xn_turned"); xT_ready = sem("xT_ready")
        q_ready = sem("q_ready"); k_ready = sem("k_ready")
        q_parts = sem("q_parts"); k_parts = sem("k_parts"); rot_ready = sem("rot_ready")
        scored = sem("scored"); sc_ready = sem("sc_ready"); prob_ready = sem("prob_ready")
        prob_turned = sem("prob_turned"); probT_ready = sem("probT_ready")
        v_made = sem("v_made"); v_ready = sem("v_ready"); y_made = sem("y_made")
        rinv_ready = sem("rinv_ready"); h1_ready = sem("h1_ready")
        f_stats = sem("f_stats"); f_mv = sem("f_mv"); f_var = sem("f_var"); f_rstd = sem("f_rstd")
        x2_ready = sem("x2_ready"); x2_turned = sem("x2_turned"); x2T_ready = sem("x2T_ready")
        mean_ready = sem("mean_ready")
        pre_made = sem("pre_made"); tw_made = sem("tw_made")
        pre_out = sem("pre_out"); tw_out = sem("tw_out")
        g_mm = sem("g_mm"); g_act = sem("g_act"); base_ready = sem("base_ready")
        a1_ready = sem("a1_ready"); l2_made = sem("l2_made"); a2_ready = sem("a2_ready")
        l3_made = sem("l3_made"); a3_ready = sem("a3_ready"); l4_made = sem("l4_made")
        zcol_made = sem("zcol_made")
        tz_ready = sem("tz_ready"); tcol_ready = sem("tcol_ready")
        cpl_ready = sem("cpl_ready"); up_ready = sem("up_ready"); ut_ready = sem("ut_ready"); ut1_ready = sem("ut1_ready"); pre_new = sem("pre_new")
        tw_new = sem("tw_new"); factor_steps = sem("factor_steps"); c3_steps = sem("c3_steps"); xf_ready = sem("xf_ready")
        factors_ready = sem("factors_ready"); mixed_by_pool = sem("mixed_by_pool"); mixed_by_act = sem("mixed_by_act")
        ab_ready = sem("ab_ready"); h_out = sem("h_out")

        def at_least(eng, s, v):
            if not (isinstance(v, int) and v <= 0):
                eng.wait_ge(s, v)

        def wait_alone(eng, s, v):
            if isinstance(v, int):
                return at_least(eng, s, v)
            v = eng.to_reg(v)
            eng.wait_ge(con_in, 16)
            eng.wait_ge(s, v)

        def phases(eng, body):
            body(-2, "D")
            body(-1, "DE")
            body(0, "DEX")
            body(1, "DEXA")
            body(2, "DEXAF")
            with eng.Fori(3, PAIRS - 2) as i:
                body(i, "DEXAF")
            body(PAIRS - 2, "EXAF")
            body(PAIRS - 1, "XAF")
            body(PAIRS, "AF")

        def starting(i):
            return isinstance(i, int) and i <= 1

        def row_of(b):
            return h[:, bass.ds(b, 1), :].rearrange("p o d -> p (o d)")

        block = ctx.enter_context(nc.Block())

        @block.sync
        def _(sp):
            sp.dma_start(ids_sb[:, :], ids).then_inc(ids_in, 16)
            sp.wait_ge(rows_in[1], 16)
            sp.dma_start(emb_sb[:, E_LNW:5 * D], emb[:, E_LNW:5 * D]).then_inc(ln_in, 16)
            sp.dma_start(con[:, :], consts).then_inc(con_in, 16)
            sp.dma_start(aw[:, :, :], attn_w).then_inc(aw_in, 16)
            sp.dma_start(fw[:, :], ffn_w).then_inc(fw_in, 16)
            pieces = [slice(4 * g, 4 * g + 4) for g in range(GROUPS - 1)] + [slice(NB - 4, NB - 2), slice(NB - 2, NB)]
            for rows in pieces:
                sp.wait_ge(h_out, 2 * rows.stop)
                sp.dma_start(out[rows].rearrange("b t d -> t b d"), h[:, rows, :]).then_inc(out_done, 16)
            sp.wait_ge(out_done, 16 * len(pieces))

        @block.gpsimd
        def _(pool):
            def gather(b):
                if b < FIRST_ROWS:
                    op = ALU.bypass
                else:
                    pool.wait_ge(prefilled, b - FIRST_ROWS + 1)
                    op = ALU.add
                pool.indirect_dma_start(
                    out=h[:, b, :], out_offset=None, in_=token_w,
                    in_offset=bass.IndirectOffsetOnAxis(ap=ids_sb[:, b:b + 1], axis=0),
                    compute_op=op,
                ).then_inc(rows_in[b] if b < 2 * FIRST_PAIRS else rest_in, 16)

            pool.wait_ge(ids_in, 16)
            for b in range(FIRST_ROWS):
                gather(b)
            later = iter(range(FIRST_ROWS, NB))
            after = {(-2, "embedding"): 2, (-1, "embedding"): 1, (0, "embedding"): 1, (1, "embedding"): 1,
                     (1, "rotate"): 2, (1, "second"): 1, (2, "second"): 2}

            def gather_more(i, stage):
                if isinstance(i, int):
                    for _ in range(after.get((i, stage), 0)):
                        gather(next(later))

            def rstd(out_r, out_b, ve, nm, done, ready):
                pool.tensor_tensor(out_r, ve[:, :], neg_half[:, :], ALU.pow).then_inc(ready, 1)
                pool.wait_ge(ready, done + 1)
                pool.tensor_tensor(out_b, nm[:, :], out_r, ALU.mult).then_inc(ready, 1)

            def attention_rstd(i):
                pool.wait_ge(a_var, 2 * (i + 2))
                at_least(pool, xn_ready, 2 * (i + 1))
                rstd(rs_a[:, :], nb_a[:, :], ve_a, nm_a, 2 * (i + 1), a_rstd)
                gather_more(i, "attention")

            def embedding_rstd(i):
                pool.wait_ge(e_var, 2 * (i + 3))
                at_least(pool, e_norm, 2 * (i + 2))
                rstd(rs_e[:, :], nb_e[:, :], ve_e, nm_e, 2 * (i + 2), e_rstd)
                gather_more(i, "embedding")

            def weigh_embedding(i):
                if isinstance(i, int):
                    pool.wait_ge(ln_in, 16)
                for j in range(2):
                    row = row_of(2 * i + 4 + j)
                    pool.wait_ge(e_norm, 2 * (i + 2) + j + 1)
                    pool.tensor_tensor(row, row, lnw, ALU.mult).then_inc(e_scaled, 1)

            def rotate(i, m):
                pool.wait_ge((q_parts, k_parts)[m], i + 1)
                if m == 0:
                    at_least(pool, scored, i)
                pool.tensor_tensor(rot[:, m, 0], tcos[:, m, 0], tsin[:, m, 1], ALU.subtract).then_inc(rot_ready, 1)
                pool.tensor_tensor(rot[:, m, 1], tcos[:, m, 1], tsin[:, m, 0], ALU.add).then_inc(rot_ready, 1)
                if m == 1:
                    gather_more(i, "rotate")

            def body(i, what):
                if starting(i) and i in (-2, 0):
                    embedding_rstd(i)
                if "E" in what:
                    attention_rstd(i)
                if starting(i) and i in (-1, 1):
                    embedding_rstd(i)
                if "X" in what:
                    rotate(i, 0)
                if "D" in what and not starting(i):
                    embedding_rstd(i)
                if "X" in what:
                    rotate(i, 1)
                if "D" in what and not starting(i):
                    weigh_embedding(i)
                if "A" in what:
                    pool.wait_ge(f_var, 2 * i)
                    cols = bass.ds(2 * i - 2, 2)
                    rstd(x2r[:, cols], x2nm[:, cols], ve_f, nm_f, 2 * (i - 1), f_rstd)
                    gather_more(i, "second")

            phases(pool, body)

            pool.wait_ge(f_rstd, 2 * PAIRS)
            for b in range(NB):
                pool.tensor_scalar(xf[:, b, :], h[:, b, :], x2r[:, b:b + 1], x2nm[:, b:b + 1],
                                   ALU.mult, ALU.add).then_inc(xf_ready, 1)

            for n in range(GROUPS):
                c = cpl[:, n % 2].rearrange("p j t -> p (j t)")
                cols = slice(n * NG, (n + 1) * NG)
                pool.wait_ge(cpl_ready, n + 1)
                at_least(pool, tw_new, n)
                pool.tensor_tensor(ut[:, 0, :], pre[:, 0, cols], c, ALU.mult).then_inc(ut_ready, 1)
                pool.wait_ge(ut1_ready, n + 1)
                pool.wait_ge(up_ready, n + 1)
                pool.wait_ge(ut_ready, n + 1)
                pool.tensor_tensor(tw[:, :, cols], tw[:, :, cols], ut[:, :, :], ALU.subtract).then_inc(tw_new, 1)

            steps = [0]

            def step(ins, wait=True):
                ins.then_inc(factor_steps, 1)
                steps[0] += 1
                if wait:
                    pool.wait_ge(factor_steps, steps[0])

            pool.wait_ge(tcol_ready, (CYCLES - 1) * GROUPS)
            pool.wait_ge(base_ready, 1)
            both = base[:, :].unsqueeze(1).broadcast_to([P, 2, NB])
            c1, c2 = ccol[:, 0, :], ccol[:, 1, :]
            step(pool.tensor_scalar(ccol[:, 0:2, :], tcol[:, 0:2, :], ar03[:, :], 1.0, ALU.mult, ALU.mult))
            step(pool.tensor_tensor(ccol[:, 0:2, :], ccol[:, 0:2, :], both, ALU.add))
            step(pool.tensor_tensor(c12[:, :], c1, c2, ALU.mult), wait=False)
            step(pool.tensor_tensor(fix[:, F_BETA, :], c1, c2, ALU.add))
            step(pool.tensor_scalar(slope[:, F_BETA, :], c12[:, :], -1.0, 1.0, ALU.mult, ALU.add), wait=False)
            step(pool.tensor_scalar(fix[:, F_NBETA, :], fix[:, F_BETA, :], -1.0, 1.0, ALU.mult, ALU.mult))
            a2col = slope[:, F_BETA, :]
            step(pool.tensor_scalar(slope[:, F_NBETA, :], a2col, -1.0, 1.0, ALU.mult, ALU.mult), wait=False)
            step(pool.tensor_tensor(fix[:, F_SCALE, :], a2col, x2r[:, :], ALU.mult), wait=False)
            step(pool.tensor_tensor(fix[:, F_BIAS, :], a2col, x2nm[:, :], ALU.mult), wait=False)
            step(pool.tensor_tensor(slope[:, F_SCALE, :], fix[:, F_NBETA, :], x2r[:, :], ALU.mult), wait=False)
            step(pool.tensor_tensor(slope[:, F_BIAS, :], fix[:, F_NBETA, :], x2nm[:, :], ALU.mult))
            pool.tensor_scalar(fix[:, F_SCALE, :], fix[:, F_SCALE, :], 1.0, 1.0, ALU.add, ALU.mult).then_inc(factors_ready, 1)

            for g in range(GROUPS):
                pool.wait_ge(ab_ready, g + 1)
                for b in range(4 * g + 2, 4 * g + 4):
                    pool.tensor_scalar(h[:, b, :], h[:, b, :], fac[:, g % 2, F_SCALE, b % 4:b % 4 + 1],
                                       fac[:, g % 2, F_BIAS, b % 4:b % 4 + 1],
                                       ALU.mult, ALU.add).then_inc(mixed_by_pool, 1)

        @block.tensor
        def _(pe):
            pe.wait_ge(con_in, 16)

            def turn_second_input(i):
                pe.wait_ge(x2_ready, 2 * (i - 1))
                if not isinstance(i, int) or i < PAIRS:
                    pe.wait_ge(xT_ready, i + 1)
                else:
                    pe.wait_ge(x2T_ready, i - 2)
                for j in range(2):
                    for a in range(2):
                        mm = pe.transpose(tr_ps[:, j, a, :], x2[:, j, a * P:(a + 1) * P], ident)
                mm.then_inc(x2_turned, 1)

            def layer1(i, w, ps, left, made):
                at_least(pe, left, i - 2)
                for m in range(2):
                    for k in range(2):
                        mm = pe.matmul(ps[:, m, :], w[:, k, m * P:(m + 1) * P],
                                       x2T[:, k, :, :].rearrange("p j t -> p (j t)"),
                                       start=(k == 0), stop=(k == 1))
                mm.then_inc(made, 1)

            def values(i):
                at_least(pe, v_ready, i)
                for j in range(2):
                    for par in range(2):
                        mm = pe.matmul(v_ps[:, j, par, :], xT[:, par, j, :], w_attn(2, par),
                                       start=True, stop=True)
                mm.then_inc(v_made, 1)

            def scores(i):
                pe.wait_ge(rot_ready, 4 * i)
                at_least(pe, probT_ready, i - 1)
                for j in range(2):
                    for par in range(2):
                        mm = pe.matmul(s_ps[:, j, :], rot[:, 0, par, j, :], rot[:, 1, par, j, :],
                                       start=(par == 0), stop=(par == 1))
                mm.then_inc(scored, 1)

            def body(i, what):
                if "X" in what:
                    pe.wait_ge(xn_ready, 2 * (i + 1))
                    at_least(pe, x2T_ready, i - 2)
                    for j in range(2):
                        for par in range(2):
                            mm = pe.transpose(tr_ps[:, j, par, :], xn[:, j, par, :], ident)
                    mm.then_inc(xn_turned, 1)
                if "A" in what and not starting(i):
                    scores(i)
                if "X" in what:
                    pe.wait_ge(xT_ready, i + 1)
                    if isinstance(i, int) and i == 0:
                        pe.wait_ge(wqkv_ready, 1)
                    for m, (ps, used, made) in enumerate(((q_ps, q_parts, q_ready), (k_ps, k_parts, k_ready))):
                        at_least(pe, used, i)
                        for par in range(2):
                            mm = pe.matmul(ps[:, par, :], w_attn(m, par),
                                           xT[:, par, :, :].rearrange("p j t -> p (j t)"),
                                           start=True, stop=True)
                        mm.then_inc(made, 1)
                if "X" in what and starting(i):
                    values(i)
                if "A" in what and starting(i):
                    scores(i)
                if "F" in what:
                    turn_second_input(i)
                if "A" in what:
                    pe.wait_ge(prob_ready, 2 * i)
                    for j in range(2):
                        mm = pe.transpose(pt_ps[:, j, :], prob[:, j, :], ident)
                    mm.then_inc(prob_turned, 1)
                if "X" in what and not starting(i):
                    values(i)
                if "A" in what:
                    pe.wait_ge(probT_ready, i)
                    pe.wait_ge(v_ready, i)
                    at_least(pe, h1_ready, 2 * (i - 1))
                    for j in range(2):
                        mm = pe.matmul(y_ps[:, j, :], probT[:, j, :], v_sb[:, j, :], start=True, stop=True)
                    mm.then_inc(y_made, 1)
                if "F" in what:
                    pe.wait_ge(x2T_ready, i - 1)
                    if isinstance(i, int) and i == 2 or not isinstance(i, int):
                        pe.wait_ge(ffn_ready, 4)
                    layer1(i, w1, pre_ps, pre_out, pre_made)
                    layer1(i, w1t, tw_ps, tw_out, tw_made)

            phases(pe, body)

            items = CYCLES * GROUPS

            def layer2(n):
                pe.wait_ge(a1_ready, n + 1)
                at_least(pe, a2_ready, n - 1)
                for k in range(2):
                    mm = pe.matmul(l2_ps[n % 2][:, :], w2[:, k, :], a1[:, n % 2, k, :],
                                   start=(k == 0), stop=(k == 1))
                mm.then_inc(l2_made, 1)

            def layer3(n):
                pe.wait_ge(a2_ready, n + 1)
                at_least(pe, a3_ready, n - 1)
                pe.matmul(l3_ps[n % 2][0:64, :], w3, a2[:, n % 2, :], start=True, stop=True).then_inc(l3_made, 1)

            def layer4(n):
                pe.wait_ge(a3_ready, n + 1)
                if n < items - GROUPS:
                    at_least(pe, tz_ready, n - 1)
                    if n == 1:
                        pe.wait_ge(pre_out, PAIRS)
                    pe.matmul(l4_ps[n % 2][:, :], w4w[:, :], a3[:, n % 2, :],
                              start=True, stop=True).then_inc(l4_made, 1)
                at_least(pe, tcol_ready, n - 1)
                if n == 0:
                    pe.wait_ge(tw_out, PAIRS)
                if n == 1:
                    pe.wait_ge(g_act, 3)
                for j in range(4):
                    mm = pe.matmul(zcol_ps[n % 2][:, j:j + 1], a3[:, n % 2, j * P:(j + 1) * P],
                                   fw[0:64, F_W4:F_W4 + 1], start=True, stop=True)
                mm.then_inc(zcol_made, 1)

            layer2(0)
            layer2(1)
            turn_second_input(PAIRS + 1)
            layer3(0)
            pe.wait_ge(x2T_ready, PAIRS)
            layer1(PAIRS + 1, w1, pre_ps, pre_out, pre_made)
            layer1(PAIRS + 1, w1t, tw_ps, tw_out, tw_made)
            pe.wait_ge(mean_ready, PAIRS)
            for k in range(2):
                mm = pe.matmul(g_ps[:, 0:NB], gw1[:, k, :], gsum[:, k, :], start=(k == 0), stop=(k == 1))
            mm.then_inc(g_mm, 1)
            layer4(0)
            pe.wait_ge(g_act, 1)
            pe.matmul(g_ps[0:64, 0:NB], gw2, g1[:, :], start=True, stop=True).then_inc(g_mm, 1)
            layer3(1)
            pe.wait_ge(g_act, 2)
            pe.matmul(g_ps[:, 0:NB], g3w[:, :], g2[:, :], start=True, stop=True).then_inc(g_mm, 1)
            layer2(2)
            for n in range(3, items + 2):
                layer4(n - 2)
                if n <= items:
                    layer3(n - 1)
                if n < items:
                    layer2(n)

        @block.scalar
        def _(act):
            act.dma_start(emb_sb[:, 0:E_LNW], emb[:, 0:E_LNW]).then_inc(emb_in, 16)
            items = CYCLES * GROUPS

            def first(n):
                g = n % GROUPS
                if n < GROUPS:
                    act.wait_ge(pre_out, 2 * (g + 1))
                else:
                    act.wait_ge(pre_new, n - GROUPS + 1)
                at_least(act, l2_made, n - 1)
                for k in range(2):
                    ins = act.activation(a1[:, n % 2, k, :], pre[:, k, g * NG:(g + 1) * NG], ACT.Gelu,
                                         bias=fw[:, F_B1 + k:F_B1 + k + 1])
                ins.then_inc(a1_ready, 1)

            def second_input(p):
                wait_alone(act, f_rstd, 2 * (p + 1))
                wait_alone(act, x2_turned, p)
                for j in range(2):
                    act.activation(x2[:, j, :], row_of(2 * p + j), ACT.Identity,
                                   bias=x2nm[:, bass.ds(2 * p + j, 1)],
                                   scale=x2r[:, bass.ds(2 * p + j, 1)]).then_inc(x2_ready, 1)

            def turned_second_input(i):
                act.wait_ge(x2_turned, i - 1)
                at_least(act, tw_made, i - 2)
                at_least(act, mean_ready, i - 2)
                act.activation(x2T[:, :, :, :], tr_ps.rearrange("p j a t -> p a j t"),
                               ACT.Copy).then_inc(x2T_ready, 1)

            def ffn_weights():
                act.wait_ge(fw_in, 16)
                act.wait_ge(con_in, 16)
                act.wait_ge(prep, 2)
                for k, col in ((0, C_SIGN), (1, C_SIGN + 1)):
                    act.activation(w1t[:, k, :], w1[:, 1 - k, :], ACT.Identity,
                                   scale=con[:, col:col + 1]).then_inc(ffn_ready, 1)
                for wide, col in ((w4w, F_W4), (g3w, F_G3)):
                    act.activation(wide[:, :], ones[:, :], ACT.Identity,
                                   scale=fw[0:64, col:col + 1]).then_inc(ffn_ready, 1)
                for dst, col, factor in ((half_b4, F_B4, 0.5), (half_gb3, F_GB3, 0.5), (ar03, F_AR, 0.3), (ar07, F_AR, 0.7)):
                    act.activation(dst[:, :], fw[:, col:col + 1], ACT.Copy, scale=factor).then_inc(scalars_ready, 1)

            def normalise_embedding(i):
                wait_alone(act, e_rstd, 2 * (i + 3))
                for j in range(2):
                    act.activation(row_of(2 * i + 4 + j), row_of(2 * i + 4 + j), ACT.Identity,
                                   bias=nb_e[:, j:j + 1], scale=rs_e[:, j:j + 1]).then_inc(e_norm, 1)

            def normalise_tokens(i):
                wait_alone(act, a_rstd, 2 * (i + 2))
                wait_alone(act, xn_turned, i + 1)
                for j in range(2):
                    act.activation(xn[:, j, :, :], row_of(2 * i + 2 + j).rearrange("p (i a) -> p a i", a=2),
                                   ACT.Identity, bias=nb_a[:, j:j + 1],
                                   scale=rs_a[:, j:j + 1]).then_inc(xn_ready, 1)

            def layer1_out(i, dst, ps, made, out_sem):
                act.wait_ge(made, i - 1)
                act.activation(dst[:, :, bass.ds((i - 2) * (2 * P), 2 * P)], ps, ACT.Copy).then_inc(out_sem, 1)

            def body(i, what):
                if "X" in what:
                    act.wait_ge(xn_turned, i + 1)
                    at_least(act, v_made, i)
                    act.activation(xT[:, :, :, :], tr_ps.rearrange("p j a t -> p a j t"),
                                   ACT.Copy).then_inc(xT_ready, 1)
                if starting(i):
                    if i in (-2, 0):
                        normalise_embedding(i)
                    if i == -2:
                        ffn_weights()
                    if "E" in what:
                        normalise_tokens(i)
                    if i == -1:
                        normalise_embedding(i)
                if "F" in what:
                    second_input(i - 2)
                if "A" in what:
                    for j in range(2):
                        act.wait_ge(sc_ready, 2 * (i - 1) + j + 1)
                        if j == 0:
                            at_least(act, prob_turned, i - 1)
                            at_least(act, rinv_ready, i - 1)
                        act.activation(prob[:, j, :], sc[:, j, :], ACT.Exp, bias=nmax[:, j:j + 1], scale=-1.0,
                                       accum_out=psum_row[:, j:j + 1]).then_inc(prob_ready, 1)
                if "F" in what:
                    turned_second_input(i)
                if "A" in what:
                    act.wait_ge(prob_turned, i)
                    at_least(act, y_made, i - 1)
                    act.activation(probT[:, :, :], pt_ps, ACT.Copy).then_inc(probT_ready, 1)
                if starting(i) and i == 1:
                    normalise_embedding(i)
                if "E" in what and not starting(i):
                    normalise_tokens(i)
                if "X" in what:
                    act.wait_ge(v_made, i + 1)
                    at_least(act, y_made, i)
                    act.activation(v_sb[:, :, :].rearrange("p j (i a) -> p j a i", a=2), v_ps,
                                   ACT.Copy).then_inc(v_ready, 1)
                if what == "AF":
                    act.wait_ge(fw_in, 16)
                    first(0)
                if "F" in what:
                    layer1_out(i, pre, pre_ps, pre_made, pre_out)
                if "D" in what and not starting(i):
                    normalise_embedding(i)
                if "F" in what:
                    layer1_out(i, tw, tw_ps, tw_made, tw_out)
            phases(act, body)

            def second(n):
                act.wait_ge(l2_made, n + 1)
                at_least(act, l3_made, n - 1)
                act.activation(a2[:, n % 2, :], l2_ps[n % 2][:, :], ACT.Gelu,
                               bias=fw[:, F_B2:F_B2 + 1]).then_inc(a2_ready, 1)

            def third(n):
                act.wait_ge(l3_made, n + 1)
                at_least(act, zcol_made, n - 1)
                act.activation(a3[:, n % 2, :], l3_ps[n % 2][0:64, :], ACT.Gelu,
                               bias=fw[0:64, F_B3:F_B3 + 1]).then_inc(a3_ready, 1)

            def last(n):
                g = n % GROUPS
                if n < items - GROUPS:
                    act.wait_ge(l4_made, n + 1)
                    at_least(act, cpl_ready, n - 1)
                    act.activation(tz[:, n % 2, :], l4_ps[n % 2][:, :], ACT.Tanh, bias=half_b4[:, :],
                                   scale=0.5).then_inc(tz_ready, 1)
                act.wait_ge(zcol_made, n + 1)
                act.activation(tcol[:, n // GROUPS, 4 * g:4 * g + 4], zcol_ps[n % 2][:, 0:4], ACT.Tanh,
                               bias=half_b4[:, :], scale=0.5).then_inc(tcol_ready, 1)

            def alpha_rows(g):
                act.wait_ge(ab_ready, g + 1)
                for b in range(4 * g, 4 * g + 2):
                    act.activation(h[:, b, :], h[:, b, :], ACT.Identity,
                                   bias=fac[:, g % 2, F_BIAS, b % 4:b % 4 + 1],
                                   scale=fac[:, g % 2, F_SCALE, b % 4:b % 4 + 1]).then_inc(mixed_by_act, 1)

            act.wait_ge(scalars_ready, 4)
            first(1)
            second_input(PAIRS - 1)
            second(0)
            turned_second_input(PAIRS + 1)
            third(0)
            second(1)
            first(2)
            layer1_out(PAIRS + 1, pre, pre_ps, pre_made, pre_out)
            layer1_out(PAIRS + 1, tw, tw_ps, tw_made, tw_out)
            act.wait_ge(g_mm, 1)
            act.activation(g1[:, :], g_ps[:, 0:NB], ACT.Gelu, bias=fw[:, F_GB1:F_GB1 + 1],
                           scale=1.0 / P).then_inc(g_act, 1)
            act.wait_ge(g_mm, 2)
            act.activation(g2[:, :], g_ps[0:64, 0:NB], ACT.Gelu,
                           bias=fw[0:64, F_GB2:F_GB2 + 1]).then_inc(g_act, 1)
            last(0)
            third(1)
            act.wait_ge(g_mm, 3)
            act.activation(tg[:, :], g_ps[:, 0:NB], ACT.Tanh, bias=half_gb3[:, :],
                           scale=0.5).then_inc(g_act, 1)
            first(3)
            second(2)
            for n in range(3, items + 2):
                last(n - 2)
                if n + 1 < items:
                    first(n + 1)
                if n <= items:
                    third(n - 1)
                if n < items:
                    second(n)
                if n - 2 >= items - GROUPS:
                    alpha_rows(n - 2 - items + GROUPS)

        @block.vector
        def _(dve):
            dve.memset(neg_half[:, :], -0.5).then_inc(prep, 1)
            dve.memset(ones[:, :], 1.0).then_inc(prep, 1)
            dve.wait_ge(ids_in, 16)
            dve.tensor_copy(typef[:, :], ids_sb[:, NB:2 * NB]).then_inc(prep, 1)
            dve.wait_ge(emb_in, 16)
            dve.tensor_tensor(pos0[:, :], emb_sb[:, E_POS:E_POS + D], emb_sb[:, E_TYPE0:E_TYPE0 + D],
                              ALU.add).then_inc(prep, 1)
            dve.tensor_tensor(tdiff[:, :], emb_sb[:, E_TYPE1:E_TYPE1 + D], emb_sb[:, E_TYPE0:E_TYPE0 + D],
                              ALU.subtract).then_inc(prep, 1)
            dve.wait_ge(prep, 5)

            def make_place(rows):
                for b in rows:
                    dve.scalar_tensor_tensor(out=place[:, b, :], in0=tdiff[:, :], scalar=typef[:, b:b + 1],
                                             in1=pos0[:, :], op0=ALU.mult, op1=ALU.add).then_inc(place_ready, 1)

            def add_place(rows):
                for b in rows:
                    dve.wait_ge(rows_in[b], 16)
                    dve.wait_ge(place_ready, b + 1)
                    dve.tensor_tensor(h[:, b, :], h[:, b, :], place[:, b, :], ALU.add).then_inc(placed, 1)

            def prefill(rows):
                for b in rows:
                    dve.scalar_tensor_tensor(out=h[:, b, :], in0=tdiff[:, :], scalar=typef[:, b:b + 1],
                                             in1=pos0[:, :], op0=ALU.mult, op1=ALU.add).then_inc(prefilled, 1)

            def attention_weights():
                dve.wait_ge(con_in, 16)
                dve.wait_ge(aw_in, 16)
                head = con[:, C_HEAD:C_HEAD + H // 2]
                dve.tensor_tensor(wqkv[:, :, :, :].rearrange("p m d i -> p (m d) i"),
                                  aw[:, :, :].rearrange("p m d -> p (m d)").unsqueeze(2).broadcast_to([P, 6 * HD, H // 2]),
                                  head.unsqueeze(1).broadcast_to([P, 6 * HD, H // 2]),
                                  ALU.mult).then_inc(wqkv_ready, 1)

            def layernorm_stats(rows, st, mv, ve, nm, stats, mvs, var, rstd_made, done):
                for j in range(2):
                    dve.bn_stats(st[:, j, :], rows[j]).then_inc(stats, 1)
                for j in range(2):
                    wait_alone(dve, stats, 2 * done + j + 1)
                    dve.bn_aggr(mv[:, j, :], st[:, j, :]).then_inc(mvs, 1)
                if isinstance(done, int) or rstd_made is f_rstd:
                    at_least(dve, rstd_made, 2 * done)
                dve.wait_ge(mvs, 2 * done + 2)
                dve.tensor_scalar(ve[:, :], mv[:, :, 1], EPS, None, ALU.add).then_inc(var, 1)
                dve.tensor_scalar(nm[:, :], mv[:, :, 0], -1.0, None, ALU.mult).then_inc(var, 1)

            def attention_stats(i):
                rows = [row_of(2 * i + 2), row_of(2 * i + 3)]
                if isinstance(i, int) and i <= 2:
                    for j in range(2):
                        dve.wait_ge(e_norm, 2 * (i + 1) + j + 1)
                        dve.tensor_tensor(rows[j], rows[j], lnw, ALU.mult).then_inc(e_scaled, 1)
                for j in range(2):
                    wait_alone(dve, e_scaled, 2 * (i + 1) + j + 1)
                    dve.tensor_tensor(rows[j], rows[j], lnb, ALU.add).then_inc(h0_ready, 1)
                wait_alone(dve, h0_ready, 2 * (i + 2))
                layernorm_stats(rows, st_a, mv_a, ve_a, nm_a, a_stats, a_mv, a_var, a_rstd, i + 1)

            def embedding_stats(i):
                if isinstance(i, int) and i < FIRST_PAIRS - 2:
                    for b in range(2 * i + 4, 2 * i + 6):
                        dve.wait_ge(rows_in[b], 16)
                        if b < FIRST_ROWS:
                            dve.wait_ge(placed, b + 1)
                else:
                    dve.wait_ge(rest_in, 16 * (NB - 2 * FIRST_PAIRS))
                layernorm_stats([row_of(2 * i + 4), row_of(2 * i + 5)], st_e, mv_e, ve_e, nm_e,
                                e_stats, e_mv, e_var, e_rstd, i + 2)

            def body(i, what):
                if starting(i):
                    if i == -2:
                        make_place(range(3))
                        add_place(range(2))
                    if i in (-2, 0):
                        embedding_stats(i)
                    if i == -2:
                        make_place(range(3, FIRST_ROWS))
                        prefill(range(FIRST_ROWS, FIRST_ROWS + 2))
                        add_place(range(2, 4))
                        attention_weights()
                        dve.wait_ge(ln_in, 16)
                    if "E" in what:
                        attention_stats(i)
                    if i in (-1, 1):
                        embedding_stats(i)
                    if i == -1:
                        prefill(range(FIRST_ROWS + 2, FIRST_ROWS + 4))
                        add_place(range(4, FIRST_ROWS))
                    if i == 0:
                        prefill(range(FIRST_ROWS + 4, FIRST_ROWS + 6))
                if "A" in what:
                    row_minima(i)
                if "E" in what and not starting(i):
                    attention_stats(i)
                if "X" in what:
                    for m, (made, parts) in enumerate(((q_ready, q_parts), (k_ready, k_parts))):
                        dve.wait_ge(made, i + 1)
                        if m == 0:
                            at_least(dve, rot_ready, 4 * i)
                        ps = banks[1 + m][:, :].rearrange("p (c t) -> p c t", c=4)
                        dve.tensor_tensor(tcos[:, m].rearrange("p a j t -> p (a j) t"), ps, cos_b, ALU.mult)
                        dve.tensor_tensor(tsin[:, m].rearrange("p a j t -> p (a j) t"), ps, sin_b,
                                          ALU.mult).then_inc(parts, 1)
                        if m == 0 and "D" in what and not starting(i):
                            embedding_stats(i)
                if starting(i) and i == 1:
                    prefill(range(FIRST_ROWS + 6, NB))
                if "A" in what:
                    dve.wait_ge(prob_ready, 2 * i)
                    dve.reciprocal(rinv[:, :], psum_row[:, :]).then_inc(rinv_ready, 1)
                    dve.wait_ge(rinv_ready, i)
                    dve.wait_ge(y_made, i)
                    mine = [row_of(2 * i - 2), row_of(2 * i - 1)]
                    for j in range(2):
                        dve.scalar_tensor_tensor(out=mine[j], in0=y_ps[:, j, :], scalar=rinv[:, j:j + 1],
                                                 in1=mine[j], op0=ALU.mult, op1=ALU.add).then_inc(h1_ready, 1)
                    wait_alone(dve, h1_ready, 2 * i)
                    layernorm_stats(mine, st_f, mv_f, ve_f, nm_f, f_stats, f_mv, f_var, f_rstd, i - 1)
                if "F" in what:
                    mean_token(i)

            def row_minima(i):
                wait_alone(dve, prob_ready, 2 * (i - 1))
                wait_alone(dve, scored, i)
                for j in range(2):
                    dve.tensor_tensor_reduce(sc[:, j, :], s_ps[:, j, :], mask, -SCORE_SCALE, 3e38,
                                             ALU.add, ALU.min, nmax[:, j:j + 1]).then_inc(sc_ready, 1)

            def mean_token(i):
                dve.wait_ge(x2T_ready, i - 1)
                dve.tensor_reduce(gsum[:, :, bass.ds(2 * i - 4, 2)], x2T[:, :, :, :], AX.X,
                                  ALU.add).then_inc(mean_ready, 1)

            phases(dve, body)
            mean_token(PAIRS + 1)

            dve.wait_ge(g_act, 3)
            dve.wait_ge(scalars_ready, 4)
            dve.tensor_scalar(base[:, :], tg[:, :], ar07[:, :], BASE_COUPLING, ALU.mult,
                              ALU.add).then_inc(base_ready, 1)
            dve.wait_ge(base_ready, 1)
            updates = (CYCLES - 1) * GROUPS

            def products(n):
                g, s = n % GROUPS, n % 2
                dve.wait_ge(tz_ready, n + 1)
                at_least(dve, up_ready, n - 1)
                at_least(dve, ut_ready, min(n - 1, GROUPS))
                dve.scalar_tensor_tensor(out=cpl[:, s], in0=tz[:, s, :].rearrange("p (j t) -> p j t", j=4),
                                         scalar=ar03[:, :], op0=ALU.mult, op1=ALU.add,
                                         in1=base[:, 4 * g:4 * g + 4].unsqueeze(2).broadcast_to([P, 4, P])
                                         ).then_inc(cpl_ready, 1)
                dve.wait_ge(cpl_ready, n + 1)
                c = cpl[:, s].rearrange("p j t -> p (j t)").unsqueeze(1).broadcast_to([P, 2, NG])
                if n < GROUPS:
                    dve.wait_ge(tw_out, 2 * (g + 1))
                else:
                    dve.wait_ge(tw_new, g + 1)
                at_least(dve, pre_new, n - 1)
                dve.tensor_tensor(up[:, s], tw[:, :, g * NG:(g + 1) * NG], c, ALU.mult).then_inc(up_ready, 1)
                if n < GROUPS:
                    at_least(dve, tw_new, n)
                    dve.tensor_tensor(ut[:, 1, :], pre[:, 1, g * NG:(g + 1) * NG], c[:, 1, :],
                                      ALU.mult).then_inc(ut1_ready, 1)

            def add(n):
                cols = slice(n % GROUPS * NG, (n % GROUPS + 1) * NG)
                if n < GROUPS:
                    dve.wait_ge(ut_ready, n + 1)
                    dve.wait_ge(ut1_ready, n + 1)
                dve.wait_ge(up_ready, n + 1)
                dve.wait_ge(a1_ready, n + 1)
                dve.tensor_tensor(pre[:, :, cols], pre[:, :, cols], up[:, n % 2], ALU.add).then_inc(pre_new, 1)

            for n in range(updates):
                products(n)
                add(n)

            dve.wait_ge(factors_ready, 1)
            steps = [0]

            def step(ins):
                ins.then_inc(c3_steps, 1)
                steps[0] += 1
                dve.wait_ge(c3_steps, steps[0])

            for g in range(GROUPS):
                q = slice(4 * g, 4 * g + 4)
                c3 = ccol[:, 2, q]
                dve.wait_ge(tcol_ready, updates + g + 1)
                step(dve.scalar_tensor_tensor(out=c3, in0=tcol[:, 2, q], scalar=ar03[:, :],
                                              in1=base[:, q], op0=ALU.mult, op1=ALU.add))
                step(dve.tensor_tensor(part[:, :, :], slope[:, :, q], c3.unsqueeze(1).broadcast_to([P, 4, 4]), ALU.mult))
                dve.tensor_tensor(fac[:, g % 2], fix[:, :, q], part[:, :, :], ALU.add).then_inc(ab_ready, 1)
                dve.wait_ge(ab_ready, g + 1)
                dve.wait_ge(xf_ready, 4 * (g + 1))
                for b in range(4 * g, 4 * g + 4):
                    if b % 4 < 2:
                        dve.wait_ge(mixed_by_act, 2 * g + b % 4 + 1)
                    else:
                        dve.wait_ge(mixed_by_pool, 2 * g + b % 4 - 1)
                    hq = h[:, b, :].rearrange("p (q f) -> p q f", q=4)
                    xq = xf[:, b, :].rearrange("p (q f) -> p q f", q=4)
                    dve.scalar_tensor_tensor(out=hq[:, 0::3, :], in0=xq[:, 2:0:-1, :],
                                             scalar=fac[:, g % 2, F_BETA, b % 4:b % 4 + 1],
                                             in1=hq[:, 0::3, :], op0=ALU.mult, op1=ALU.add).then_inc(h_out, 1)
                    dve.scalar_tensor_tensor(out=hq[:, 1:3, :], in0=xq[:, 3::-3, :],
                                             scalar=fac[:, g % 2, F_NBETA, b % 4:b % 4 + 1],
                                             in1=hq[:, 1:3, :], op0=ALU.mult, op1=ALU.add).then_inc(h_out, 1)


def _constants():
    c = np.zeros((P, C_END), np.float32)
    c[:, C_IDENT:C_IDENT + P] = np.eye(P, dtype=np.float32)
    inv_freq = (np.float32(1.0) / np.float32(10000.0) ** (np.arange(P, dtype=np.float32) / np.float32(P)))
    angle = inv_freq.astype(np.float32)[:, None] * np.arange(P, dtype=np.float32)[None, :]
    c[:, C_COS:C_COS + P] = np.cos(angle)
    c[:, C_SIN:C_SIN + P] = np.sin(angle)
    c[:, C_MASK:C_MASK + P] = np.where(np.tril(np.ones((P, P), bool)), 0.0, MASKED)
    c[:, C_HEAD:C_HEAD + H // 2] = (np.arange(P)[:, None] % (H // 2)) == np.arange(H // 2)[None, :]
    c[:, C_SIGN] = np.where(np.arange(P) < 64, -1.0, 1.0)
    c[:, C_SIGN + 1] = -c[:, C_SIGN]
    return c


def kernel(**inputs):
    import concourse.bacc as bacc
    from concourse.bass_utils import run_bass_kernel_spmd

    a = {k: np.asarray(v) for k, v in inputs.items()}
    ids = np.concatenate([a["x"].T, a["mask_BS_i1_0"].T], axis=1)

    def rows(v):
        return np.broadcast_to(v[None, :], (P, v.shape[0]))

    emb = np.concatenate([a["L0_tok_pos_W"], rows(a["L0_tok_type_W"][0]), rows(a["L0_tok_type_W"][1]),
                          rows(a["L0_tok_ln_w"]), rows(a["L0_tok_ln_b"])], axis=1)
    attn = np.stack([a["L0_attn_w_" + m].reshape(HD, HD, H // 2, 2).transpose(0, 2, 3, 1) for m in "qkv"], axis=2)
    attn = attn.reshape(P, 6, HD)

    f = np.zeros((P, F_END), np.float32)
    w1, w2, gw1 = a["L0_ffn_cn_w1"], a["L0_ffn_cn_w2"], a["L0_ffn_gc_w1"]
    for k in range(2):
        f[:, F_W1 + k * D:F_W1 + (k + 1) * D] = w1[k * P:(k + 1) * P]
        f[:, F_W2 + k * P:F_W2 + (k + 1) * P] = w2[k * P:(k + 1) * P]
        f[:, F_G1 + k * P:F_G1 + (k + 1) * P] = gw1[k * P:(k + 1) * P]
        f[:, F_B1 + k] = a["L0_ffn_cn_b1"][k * P:(k + 1) * P]
    f[:, F_W3:F_W3 + 64] = a["L0_ffn_cn_w3"]
    f[:, F_G2:F_G2 + 64] = a["L0_ffn_gc_w2"]
    f[0:64, F_W4] = a["L0_ffn_cn_w4"][:, 0]
    f[0:64, F_G3] = a["L0_ffn_gc_w3"][:, 0]
    f[:, F_B2] = a["L0_ffn_cn_b2"]
    f[0:64, F_B3] = a["L0_ffn_cn_b3"]
    f[:, F_B4] = a["L0_ffn_cn_b4"][0]
    f[:, F_GB1] = a["L0_ffn_gc_b1"]
    f[0:64, F_GB2] = a["L0_ffn_gc_b2"]
    f[:, F_GB3] = a["L0_ffn_gc_b3"][0]
    f[:, F_AR] = a["L0_ffn_adaptive_range"][0]

    arrays = {"ids": ids, "emb": emb, "consts": _constants(), "attn_w": attn, "ffn_w": f,
              "token_w": a["L0_tok_token_W"]}
    arrays = {k: np.ascontiguousarray(v) for k, v in arrays.items()}
    nc = bacc.Bacc("TRN2", target_bir_lowering=False, num_devices=1)
    args = [nc.dram_tensor(k, v.shape, mybir.dt.from_np(v.dtype), kind="ExternalInput").ap()
            for k, v in arrays.items()]
    out = nc.dram_tensor("out", (NB, P, D), F32, kind="ExternalOutput").ap()
    tower(nc, *args, out)
    r = run_bass_kernel_spmd(nc, [arrays], core_ids=[0])
    return r.results[0]["out"]
```
